# Optimizing a Trainium2 kernel written in Bass

```python
import numpy as np
import jax
import jax.numpy as jnp

def _softmax(x, axis=-1):
    return jax.nn.softmax(x, axis=axis)

def _gelu(x):
    return jax.nn.gelu(x, approximate=True)

def _silu(x):
    return jax.nn.silu(x)

def _sigmoid(x):
    return jax.nn.sigmoid(x)

def _layernorm(x, axis=-1, eps=1e-05):
    m = jnp.mean(x, axis=axis, keepdims=True)
    v = jnp.var(x, axis=axis, keepdims=True)
    return (x - m) / jnp.sqrt(v + eps)

def _scatter_add(tgt, idx, src, axis=0):
    return tgt.at[idx].add(src)

def _segment_sum(src, seg, n):
    return jax.ops.segment_sum(src, seg, n)
kernel_name = 'mk_gnn_resnorm_d1_gnn_r8_51b17e'

def setup_inputs(seed: int=0):
    np.random.seed(seed)
    _w = jnp.asarray

    def _rec_inputs():
        import jax
        import jax.numpy as jnp
        _gk = jax.random.key(seed)
        x = -8.776e-05 + 1 * jax.random.normal(jax.random.fold_in(_gk, 1), (12500, 128), jnp.float32)
        src = jax.random.randint(jax.random.fold_in(_gk, 2), (400000,), 0, 12500, jnp.int32)
        dst = jnp.minimum((12500 * jax.random.uniform(jax.random.fold_in(_gk, 3), (400000,)) ** 2.0).astype(jnp.int32), 99999)
        _o = jnp.argsort(dst, stable=True)
        src = src[_o]
        dst = dst[_o]
        edge_attr_20 = jax.random.uniform(jax.random.fold_in(_gk, 12), (400000, 20), jnp.float32, 0.0, 1)
        edge_weight = jax.random.uniform(jax.random.fold_in(_gk, 13), (400000,), jnp.float32, 0.0, 0.999998)
        return (x, src, dst, edge_attr_20, edge_weight)
    x, src, dst, edge_attr_20, edge_weight = _rec_inputs()

    def _L0_gnn_setup():
        import jax, jax.numpy as jnp
        import numpy as np
        import math
        LOG2 = math.log(2.0)

        def shifted_softplus(x):
            return jax.nn.softplus(x) - LOG2
        key = jax.random.key(seed)
        ks = jax.random.split(key, 12)
        n_atoms, n_pairs = (5000, 80000)
        d_basis, d_filt, n_rbf = (128, 128, 20)
        x = jax.random.normal(ks[0], (n_atoms, d_basis), dtype=jnp.float32)
        f_ij = jax.random.uniform(ks[1], (n_pairs, n_rbf), dtype=jnp.float32)
        idx_i = jax.random.randint(ks[2], (n_pairs,), 0, n_atoms)
        idx_j = jax.random.randint(ks[3], (n_pairs,), 0, n_atoms)
        rcut_ij = jax.random.uniform(ks[4], (n_pairs,), dtype=jnp.float32)
        s_in = 1.0 / math.sqrt(d_basis)
        s_f = 1.0 / math.sqrt(n_rbf)
        s_out = 1.0 / math.sqrt(d_filt)
        W_in = jax.random.uniform(ks[5], (d_filt, d_basis), minval=-s_in, maxval=s_in)
        b_in = jax.random.uniform(ks[6], (d_filt,), minval=-s_in, maxval=s_in)
        W_f = jax.random.uniform(ks[7], (d_filt, n_rbf), minval=-s_f, maxval=s_f)
        b_f = jax.random.uniform(ks[8], (d_filt,), minval=-s_f, maxval=s_f)
        W_out = jax.random.uniform(ks[9], (d_basis, d_filt), minval=-s_out, maxval=s_out)
        b_out = jax.random.uniform(ks[10], (d_basis,), minval=-s_out, maxval=s_out)
        return {'x': x, 'f_ij': f_ij, 'idx_i': idx_i, 'idx_j': idx_j, 'rcut_ij': rcut_ij, 'W_in': W_in, 'b_in': b_in, 'W_f': W_f, 'b_f': b_f, 'W_out': W_out, 'b_out': b_out}
    _L0_gnn_all = _L0_gnn_setup()
    _L0_gnn_in = {k: v for k, v in _L0_gnn_all.items() if k in ('W_in', 'b_in', 'W_f', 'b_f', 'W_out', 'b_out')}
    del _L0_gnn_all
    return {'x': x, 'src': src, 'dst': dst, 'edge_attr_20': edge_attr_20, 'edge_weight': edge_weight, 'L0_gnn_W_in': _L0_gnn_in['W_in'], 'L0_gnn_b_in': _L0_gnn_in['b_in'], 'L0_gnn_W_f': _L0_gnn_in['W_f'], 'L0_gnn_b_f': _L0_gnn_in['b_f'], 'L0_gnn_W_out': _L0_gnn_in['W_out'], 'L0_gnn_b_out': _L0_gnn_in['b_out']}

def reference(x, src, dst, edge_attr_20, edge_weight, L0_gnn_W_in, L0_gnn_b_in, L0_gnn_W_f, L0_gnn_b_f, L0_gnn_W_out, L0_gnn_b_out):
    import jax
    import jax.numpy as jnp

    def _L0_gnn_ref(x, f_ij, idx_i, idx_j, rcut_ij, W_in, b_in, W_f, b_f, W_out, b_out):
        import jax, jax.numpy as jnp
        import numpy as np
        import math
        LOG2 = math.log(2.0)

        def shifted_softplus(x):
            return jax.nn.softplus(x) - LOG2
        n_atoms = x.shape[0]
        h = x @ W_in.T + b_in
        Wij = shifted_softplus(f_ij @ W_f.T + b_f) * rcut_ij[:, None]
        x_ij = h[idx_j] * Wij
        agg = jax.ops.segment_sum(x_ij, idx_i, num_segments=n_atoms)
        return shifted_softplus(agg @ W_out.T + b_out)
    x = _layernorm(x + _L0_gnn_ref(x, edge_attr_20, src, dst, edge_weight, L0_gnn_W_in, L0_gnn_b_in, L0_gnn_W_f, L0_gnn_b_f, L0_gnn_W_out, L0_gnn_b_out), axis=-1)
    return x

_drawn_inputs = setup_inputs


def setup_inputs(seed=0):
    import zlib

    import numpy as np

    out = dict(_drawn_inputs(seed))
    spreads = {}
    factors = {}
    for name, (base, spread) in spreads.items():
        noise = np.random.default_rng([zlib.crc32(name.encode()), seed]).standard_normal(out[name].shape)
        drawn = base * np.exp(spread * noise) if base else spread * noise
        out[name] = jnp.asarray(drawn.astype(out[name].dtype))
    for name, factor in factors.items():
        out[name] = (out[name] * factor).astype(out[name].dtype)
    return out
```

```python
from contextlib import ExitStack

import concourse.bass as bass
from concourse import mybir

ALU = mybir.AluOpType
ACT = mybir.ActivationFunctionType
AX_X = mybir.AxisListType.X
F32 = mybir.dt.float32
BF16 = mybir.dt.bfloat16
I32 = mybir.dt.int32

P = 128
QUAD = 4
QE = QUAD * P
GROUP = 2
GT = GROUP * QUAD
GE = GROUP * QE
REPLICAS = QUAD
EPS = 1e-5
C_SRC, C_WEIGHT, C_DUMMY, C_NODE = 0, GT, 2 * GT, 3 * GT
COLS = 3 * GT + 1
CREDIT = 4
HS = 5


def after(k):
    return k + CREDIT + 1


def quad_of(i, j):
    return i * (2 * GROUP) + j


def group_of(i, j):
    return i * 2 + j // GROUP


def prepare(nc, t):
    A_, S = t["dram"], t["sbuf"]
    cols_all, dst_all, ident, tri = S["cols_all"], S["dst_all"], S["ident"], S["tri"]
    nodes_pad, tiles, groups = t["nodes_pad"], t["tiles"], t["groups"]
    blocks = -(-groups // P)
    hi_mask = (-(-t["nodes"] // P) * P - 1)
    hi_mask = (1 << hi_mask.bit_length()) - P
    nq = nodes_pad // QE
    passes = nq // HS
    NA = A_["w_fT"].shape[0]
    assert nq % HS == 0 and hi_mask < (1 << 15)

    with ExitStack() as ctx:
        def sb(name, shape, dt):
            return ctx.enter_context(nc.sbuf_tensor(f"{name}_sb", shape, dt))

        def sem(name):
            return ctx.enter_context(nc.semaphore(f"{name}_sem"))

        nat = sb("nat", [P, 2, tiles], I32)
        hi_int = sb("hi_int", [P, tiles], I32)
        hi_row = sb("hi_row", [P, 2, tiles], BF16)
        lo_row = sb("lo_row", [P, 2, tiles], BF16)
        src_col = sb("src_col", [P, tiles], I32)
        w_col = sb("w_col", [P, tiles], F32)
        dst_g = sb("dst_g", [P, blocks, GE], I32)
        least = sb("least", [P, blocks], F32)
        most = sb("most", [P, blocks], F32)
        span = sb("span", [P, blocks], F32)
        wide = sb("wide", [P, blocks], F32)
        wide_any = sb("wide_any", [P, 1], F32)
        base_int = sb("base_int", [P, blocks], I32)
        base_bc = sb("base_bc", [P, groups], I32)
        part_i = sb("part_i", [P, 1], I32)
        part = sb("part", [P, 1], F32)
        dummy = sb("dummy_row", [P, 1], F32)
        ones_col = sb("ones_col", [P, 1], F32)
        ones_sq = sb("ones_sq", [P, P], F32)
        zeros = sb("zeros", [P, nodes_pad // 8], F32)
        xT = sb("xT", [P, HS, QE], F32)
        h_sb = sb("h_sb", [P, HS, QE], F32)
        w_in = sb("w_in", [P, P], F32)
        b_in = sb("b_in", [P, P], F32)
        h_ps = ctx.enter_context(nc.psum_tensor("h_ps", [P, HS, QE], F32))
        flag_ps = ctx.enter_context(nc.psum_tensor("flag_ps", [P, QE], F32))

        dstg_in, nat_in, dnat_in = sem("dstg_in"), sem("nat_in"), sem("dnat_in")
        col_in, w_in_sem, wts_in, tab_in = sem("col_in"), sem("w_in_sem"), sem("wts_in"), sem("tab_in")
        xT_in = [sem(f"xT_in{s}") for s in range(HS)]
        h_out = [sem(f"h_out{s}") for s in range(HS)]
        rows_out, base_out, base_in, basebc_in = (sem("rows_out"), sem("base_out"), sem("base_in"),
                                                  sem("basebc_in"))
        zeroed, zeros_set, part_set, dummy_set = sem("zeroed"), sem("zeros_set"), sem("part_set"), sem("dummy_set")
        consts_set, lims_set, lims_done, span_done = (sem("consts_set"), sem("lims_set"), sem("lims_done"),
                                                      sem("span_done"))
        base_done, flag_mm, flag_done, hi_masked = sem("base_done"), sem("flag_mm"), sem("flag_done"), sem("hi_masked")
        hi_done, lo_done, cols_set, h_mm, h_done = (sem("hi_done"), sem("lo_done"), sem("cols_set"), sem("h_mm"),
                                                    sem("h_done"))
        iota_done, attr_ones, sel_zero, sel_set = (sem("iota_done"), sem("attr_ones"), sem("sel_zero"),
                                                   sem("sel_set"))
        wf_zero, wf_in = sem("wf_zero"), sem("wf_in")
        masks_base, masks_done, weights_set = sem("masks_base"), sem("masks_done"), sem("weights_set")

        block = ctx.enter_context(nc.Block())

        @block.sync
        def _(sp):
            for b in range(blocks):
                n = min(P, groups - b * P)
                sp.dma_start(dst_g[0:n, b, :], A_["dst_g"][b * P:b * P + n]).then_inc(dstg_in, 16)
            sp.dma_start(w_in[:], A_["w_inT"]).then_inc(wts_in, 16)
            sp.dma_start(b_in[:], A_["b_in"]).then_inc(wts_in, 16)
            sp.dma_start(nat[:, 0, :], A_["src_nat"]).then_inc(nat_in, 16)
            sp.dma_start(nat[:, 1, :], A_["dst_nat"]).then_inc(dnat_in, 16)
            sp.dma_start(src_col[:], A_["src_col"]).then_inc(col_in, 16)
            sp.dma_start(w_col[:], A_["w_col"]).then_inc(w_in_sem, 16)
            sp.dma_start(dst_all[:], A_["dst_col"]).then_inc(tab_in, 16)
            sp.wait_ge(wf_zero, 1)
            for q in range(QUAD):
                sl = slice(q * P, (q + 1) * P)
                sp.dma_start(S["w_f"][q * NA:(q + 1) * NA, sl], A_["w_fT"]).then_inc(wf_in, 16)
                sp.dma_start(S["w_f"][QUAD * NA:QUAD * NA + 1, sl], A_["b_f"]).then_inc(wf_in, 16)
            sp.dma_start(S["w_out"][:], A_["w_outT"]).then_inc(tab_in, 16)
            sp.dma_start(S["b_out"][:], A_["b_out"]).then_inc(tab_in, 16)

            def load_x(i, s, again):
                if again:
                    sp.wait_ge(h_mm, i * HS + (s + 1 - HS))
                sp.dma_start(xT[:, s, :], A_["xT"][:, bass.ds(i * (HS * QE) + s * QE, QE)]).then_inc(xT_in[s], 16)

            for s in range(HS):
                load_x(0, s, False)
            sp.wait_ge(base_done, 1)
            for b in range(blocks):
                n = min(P, groups - b * P)
                sp.dma_start(A_["bases"][b * P:b * P + n], base_int[0:n, b:b + 1]).then_inc(base_out, 16)
            with sp.Fori(1, passes) as i:
                for s in range(HS):
                    load_x(i, s, True)
            sp.wait_ge(base_out, 16 * blocks)
            bases_row = A_["bases"].rearrange("g a -> a g")
            sp.dma_start(S["base_row"][:], bases_row[:, 0:groups]).then_inc(base_in, 16)
            sp.dma_start(base_bc[:], bases_row[:, 0:groups].broadcast_to([P, groups])).then_inc(basebc_in, 16)
            sp.wait_ge(hi_done, 2)
            sp.wait_ge(lo_done, 2)
            for a in range(2):
                for r, half in ((2 * a, hi_row), (2 * a + 1, lo_row)):
                    sp.dma_start(A_["rows"][r].rearrange("(p c) -> p c", p=P), half[:, a, :]).then_inc(rows_out, 16)
            sp.wait_ge(rows_out, 64)
            sp.wait_ge(base_in, 16)
            sp.wait_ge(tab_in, 48)
            sp.wait_ge(wf_in, 32 * QUAD)

        @block.gpsimd
        def _(pool):
            nc.gpsimd.memset(zeros[:], 0.0).then_inc(zeros_set, 1)
            nc.gpsimd.iota(part_i[:], pattern=[[0, 1]], base=0, channel_multiplier=1).then_inc(iota_done, 1)
            nc.gpsimd.memset(ones_sq[:], 1.0).then_inc(masks_base, 1)
            pool.wait_ge(zeros_set, 1)
            step = nodes_pad // 8
            for q in range(8):
                for r in range(REPLICAS):
                    flat = A_["agg"][r].rearrange("(p a) f -> p (a f)", p=P)
                    n = nodes_pad // 8
                    pool.dma_start(flat[:, q * n:(q + 1) * n], zeros[:]).then_inc(zeroed, 16)
            pool.wait_ge(masks_base, 1)
            nc.gpsimd.affine_select(out=tri[:], in_=ones_sq[:], compare_op=ALU.is_ge, fill=0.0, base=0,
                                    pattern=[[-1, P]], channel_multiplier=1).then_inc(masks_done, 1)
            nc.gpsimd.affine_select(out=ident[:], in_=ones_sq[:], compare_op=ALU.is_equal, fill=0.0, base=0,
                                    pattern=[[-1, P]], channel_multiplier=1).then_inc(masks_done, 1)
            pool.wait_ge(w_in_sem, 16)
            nc.gpsimd.tensor_copy(cols_all[:, :, C_WEIGHT:C_WEIGHT + GT],
                                  w_col[:].rearrange("p (g t) -> p g t", t=GT)).then_inc(weights_set, 1)
            pool.wait_ge(weights_set, 1)
            pool.wait_ge(masks_done, 2)
            pool.wait_ge(zeroed, 16 * 8 * REPLICAS)

        @block.scalar
        def _(act):
            def store_h(i, s):
                act.wait_ge(h_done, i * HS + (s + 1))
                rows = A_["h"][bass.ds(i * (HS * QE) + s * QE, QE)].rearrange("(p t) f -> p (t f)", t=QUAD)
                act.dma_start(rows, h_sb[:, s, :]).then_inc(h_out[s], 16)

            with act.Fori(0, passes) as i:
                for s in range(HS):
                    store_h(i, s)
            for a in range(2):
                act.wait_ge(hi_masked, a + 1)
                nc.scalar.copy(hi_row[:, a, :], hi_int[:]).then_inc(hi_done, 1)
            for s in range(HS):
                act.wait_ge(h_out[s], 16 * passes)

        @block.tensor
        def _(pe):
            pe.wait_ge(wts_in, 32)

            def products(i, s, again):
                pe.wait_ge(xT_in[s], i * 16 + 16)
                if again:
                    pe.wait_ge(h_done, i * HS + (s + 1 - HS))
                x_s = xT[:, s, :].rearrange("k (p t) -> k p t", t=QUAD)
                for q in range(QUAD):
                    mm = nc.tensor.matmul(h_ps[:, s, q * P:(q + 1) * P], x_s[:, :, q], w_in[:], start=True, stop=True)
                mm.then_inc(h_mm, 1)

            for s in range(HS):
                products(0, s, False)
            with pe.Fori(1, passes) as i:
                for s in range(HS):
                    products(i, s, True)
            pe.wait_ge(span_done, 3)
            nc.tensor.matmul(flag_ps[0:1, 0:1], wide_any[:], ones_col[:], start=True, stop=True).then_inc(flag_mm, 1)

        @block.vector
        def _(dve):
            nc.vector.memset(S["w_f"][:], 0.0).then_inc(wf_zero, 1)
            nc.vector.memset(least[:], 0.0).then_inc(lims_set, 1)
            nc.vector.memset(most[:], 0.0).then_inc(lims_set, 1)
            nc.vector.memset(ones_col[:], 1.0)
            nc.vector.memset(S["ones_row"][:], 1.0)
            nc.vector.memset(S["half"][:], 0.5)
            nc.vector.memset(S["minus_half"][:], -0.5)
            nc.vector.memset(S["attr"][:], 1.0)
            nc.vector.memset(S["sel_src"][:], 0.0).then_inc(sel_zero, 1)
            nc.vector.memset(S["sel_dst"][:], 1.0).then_inc(sel_zero, 1)
            dve.wait_ge(sel_zero, 2)
            nc.vector.memset(S["sel_src"][0:2, :], 1.0)
            nc.vector.memset(S["sel_dst"][0:2, :], 0.0).then_inc(sel_set, 1)
            dve.wait_ge(dstg_in, 16 * blocks)
            dve.wait_ge(lims_set, 2)
            for b in range(blocks):
                n = min(P, groups - b * P)
                nc.vector.tensor_reduce(least[0:n, b:b + 1], dst_g[0:n, b, :], AX_X, ALU.min).then_inc(lims_done, 1)
                nc.vector.tensor_reduce(most[0:n, b:b + 1], dst_g[0:n, b, :], AX_X, ALU.max).then_inc(lims_done, 1)
            dve.wait_ge(lims_done, 2 * blocks)
            nc.vector.tensor_copy(base_int[:], least[:]).then_inc(base_done, 1)
            nc.vector.tensor_tensor(span[:], most[:], least[:], ALU.subtract).then_inc(span_done, 1)
            dve.wait_ge(span_done, 1)
            nc.vector.tensor_scalar(wide[:], span[:], float(P - 1), None, ALU.is_gt).then_inc(span_done, 1)
            dve.wait_ge(span_done, 2)
            nc.vector.tensor_reduce(wide_any[:], wide[:], AX_X, ALU.add).then_inc(span_done, 1)

            def split(a, arrived):
                dve.wait_ge(arrived, 16)
                if a:
                    dve.wait_ge(hi_done, a)
                nc.vector.tensor_scalar(hi_int[:], nat[:, a, :], hi_mask, None, ALU.bitwise_and).then_inc(hi_masked, 1)
                dve.wait_ge(hi_masked, a + 1)
                nc.vector.tensor_tensor(lo_row[:, a, :], nat[:, a, :], hi_int[:], ALU.subtract).then_inc(lo_done, 1)

            def add_bias(i, s, again):
                dve.wait_ge(h_mm, i * HS + (s + 1))
                if again:
                    dve.wait_ge(h_out[s], i * 16)
                nc.vector.tensor_tensor(h_sb[:, s, :].rearrange("p (t f) -> p t f", t=QUAD),
                                        h_ps[:, s, :].rearrange("p (t f) -> p t f", t=QUAD),
                                        b_in[:].rearrange("p (a f) -> p a f", a=1).broadcast_to([P, QUAD, P]),
                                        ALU.add).then_inc(h_done, 1)

            dve.wait_ge(wts_in, 32)
            for s in range(HS):
                add_bias(0, s, False)
            with dve.Fori(1, passes) as i:
                for s in range(HS):
                    add_bias(i, s, True)
            split(0, nat_in)
            dve.wait_ge(iota_done, 1)
            nc.vector.tensor_copy(part[:], part_i[:]).then_inc(part_set, 1)
            dve.wait_ge(part_set, 1)
            nc.vector.tensor_scalar(dummy[:], part[:], float(t["nodes"]), None, ALU.add).then_inc(dummy_set, 1)
            dve.wait_ge(col_in, 16)
            nc.vector.tensor_copy(cols_all[:, :, C_SRC:C_SRC + GT],
                                  src_col[:].rearrange("p (g t) -> p g t", t=GT)).then_inc(cols_set, 1)
            dve.wait_ge(dummy_set, 1)
            nc.vector.tensor_scalar(cols_all[:, :, C_DUMMY:C_DUMMY + GT],
                                    src_col[:].rearrange("p (g t) -> p g t", t=GT), -1.0, dummy[:, 0:1],
                                    ALU.mult, ALU.add).then_inc(cols_set, 1)
            split(1, dnat_in)
            dve.wait_ge(flag_mm, 1)
            nc.vector.tensor_copy(S["flag"][:], flag_ps[0:1, 0:1]).then_inc(flag_done, 1)
            dve.wait_ge(basebc_in, 16)
            nc.vector.tensor_scalar(cols_all[:, :, C_NODE], base_bc[:], part[:, 0:1], None,
                                    ALU.add).then_inc(cols_set, 1)
            dve.wait_ge(cols_set, 3)
            dve.wait_ge(flag_done, 1)
            dve.wait_ge(sel_set, 1)


def edges(nc, t):
    A_, S = t["dram"], t["sbuf"]
    cols_all, dst_all, ident, tri = S["cols_all"], S["dst_all"], S["ident"], S["tri"]
    groups = t["groups"]
    quads = groups * GROUP
    passes = (groups - 1) // 2
    rest = quads - 4 * passes

    with ExitStack() as ctx:
        def sb(name, shape, dt):
            return ctx.enter_context(nc.sbuf_tensor(f"{name}_sb", shape, dt))

        def psum(name, shape):
            return ctx.enter_context(nc.psum_tensor(name, shape, F32))

        def sem(name):
            return ctx.enter_context(nc.semaphore(f"{name}_sem"))

        attr = S["attr"]
        KA = attr.shape[0]
        rows = sb("rows", [4, 2, GE], BF16)
        window = sb("window", [P, 2, P], F32)
        cols = sb("cols", [P, 2, COLS], F32)
        dst_i = sb("dst_i", [P, 2, GT], I32)
        onehot = sb("onehot", [P, 2, QE], F32)
        merge = sb("merge", [P, 2, QE], F32)
        count = sb("count", [P, 2, QUAD], F32)
        moved = sb("moved", [P, 2, QUAD], F32)
        target = sb("target", [P, 4, QUAD], I32)
        size = sb("size", [P, 2, QE], F32)
        expo = sb("expo", [P, 2, QE], F32)
        logp = sb("logp", [P, 2, QE], F32)
        filt = sb("filt", [P, QE], F32)
        gath = sb("gath", [P, 2, QE], F32)
        msg = sb("msg", [P, 2, QE], F32)
        stage = sb("stage", [P, 4, QE], F32)
        src_ps = psum("src_ps", [P, QE])
        dst_ps = psum("dst_ps", [P, QE])
        filt_ps = psum("filt_ps", [P, 2, QE])
        gath_ps = psum("gath_ps", [P, 2, QE])
        sum_ps = psum("sum_ps", [P, 2, QE])

        loads_in = [sem(f"loads_in{s}") for s in range(2)]
        gathered = [sem(f"gathered{s}") for s in range(2)]
        scattered = [sem(f"scattered{r}") for r in range(REPLICAS)]
        spread_done = sem("spread_done")
        onehot_done = sem("onehot_done")
        merge_done = sem("merge_done")
        target_done = sem("target_done")
        gather_done = sem("gather_done")
        linear_done = sem("linear_done")
        size_done, exp_done, log_done = sem("size_done"), sem("exp_done"), sem("log_done")
        filt_done = sem("filt_done")
        msg_done = sem("msg_done")
        sum_done = sem("sum_done")
        stage_done = sem("stage_done")
        landed = sem("landed")
        rows_asked = sem("rows_asked")
        moved_done = sem("moved_done")
        cols_done = sem("cols_done")

        block = ctx.enter_context(nc.Block())

        def both_ways(eng, body):
            wide = eng.value_load(S["flag"][0:1, 0:1], min_val=0, max_val=groups)
            with eng.If(wide == 0):
                body(True)
            with eng.Else():
                body(False)

        def steps(eng, step, local, head=()):
            for j in head:
                step(0, j, local)
            with eng.Fori(0, passes) as i:
                for j in range(4):
                    step(i, j, local)
            for j in range(rest):
                step(passes, j, local, last=True)

        def beyond(j, last):
            return last and j >= rest

        @block.sync
        def _(sp):
            def load(i, g, local):
                s = g % 2
                group = i * 2 + g
                sp.wait_ge(linear_done, after((group - 2) * GROUP + 1))
                sp.wait_ge(spread_done, after((group - 2) * GROUP + 1))
                sp.dma_start(attr[0:KA - 1, s, :], A_["attrT"][:, bass.ds(group * (GROUP * P), GROUP * P)]
                             ).then_inc(loads_in[s], 16)
                sp.dma_start(rows[:, s, :], A_["rows"][:, bass.ds(group * GE, GE)]).then_inc(loads_in[s], 16)
                if local:
                    sp.wait_ge(gather_done, after((group - 2) * GROUP + 1))
                    base = sp.value_load(S["base_row"][0:1, bass.ds(group, 1)], min_val=0, max_val=t["nodes"] - 1)
                    sp.dma_start(window[:, s, :], A_["h"][bass.ds(base, P)]).then_inc(loads_in[s], 16)

            def body(local):
                with sp.Fori(0, passes) as i:
                    for g in range(2):
                        load(i, g, local)
                for g in range(rest // GROUP):
                    load(passes, g, local)

            both_ways(sp, body)

        def loads(local):
            return 48 if local else 32

        @block.tensor
        def _(pe):
            for s in (spread_done, gather_done, linear_done, sum_done):
                pe.sem_inc(s, CREDIT)

            def arrived(i, j, local):
                pe.wait_ge(loads_in[(j // GROUP) % 2], (i + (j // GROUP) // 2 + 1) * loads(local))

            def spread(i, j, local):
                k, g, e = quad_of(i, j), (j // GROUP) % 2, (j % GROUP) * QE
                arrived(i, j, local)
                pe.wait_ge(merge_done, after(k - 1))
                nc.tensor.matmul(src_ps[:], S["sel_src"][:], rows[:, g, e:e + QE], start=True, stop=True)
                if local:
                    pe.wait_ge(onehot_done, after(k - 1))
                mm = nc.tensor.matmul(dst_ps[:], S["sel_dst"][:], rows[:, g, e:e + QE], start=True, stop=True)
                mm.then_inc(spread_done, 1)

            def linear(i, j, local):
                k, g, e = quad_of(i, j), (j // GROUP) % 2, (j % GROUP) * P
                arrived(i, j, local)
                pe.wait_ge(filt_done, after(k - 2))
                mm = nc.tensor.matmul(filt_ps[:, j % 2, :], attr[:, g, e:e + P], S["w_f"][:], start=True, stop=True)
                mm.then_inc(linear_done, 1)

            def gather(i, j, local):
                k, g = quad_of(i, j), (j // GROUP) % 2
                pe.wait_ge(onehot_done, after(k))
                pe.wait_ge(msg_done, after(k - 2))
                for q in range(QUAD):
                    mm = nc.tensor.matmul(gath_ps[:, j % 2, q * P:(q + 1) * P], onehot[:, j % 2, q * P:(q + 1) * P],
                                          window[:, g, :], start=True, stop=True)
                mm.then_inc(gather_done, 1)

            def merge_sources(i, j):
                k = quad_of(i, j)
                pe.wait_ge(merge_done, after(k))
                pe.wait_ge(msg_done, after(k))
                pe.wait_ge(stage_done, after(k - 2))
                for q in range(QUAD):
                    sl = slice(q * P, (q + 1) * P)
                    mm = nc.tensor.matmul(sum_ps[:, j % 2, sl], merge[:, j % 2, sl], msg[:, j % 2, sl],
                                          start=True, stop=True)
                mm.then_inc(sum_done, 1)

            def step(i, j, local, last=False):
                if local and not beyond(j + 1, last):
                    gather(i, j + 1, local)
                if not beyond(j + 2, last):
                    spread(i, j + 2, local)
                    linear(i, j + 2, local)
                if j >= 0:
                    merge_sources(i, j)

            def body(local):
                spread(0, 0, local)
                linear(0, 0, local)
                steps(pe, step, local, head=(-1,))

            both_ways(pe, body)

        @block.vector
        def _(dve):
            for s in (onehot_done, merge_done, target_done, filt_done, msg_done, moved_done, cols_done):
                dve.sem_inc(s, CREDIT)

            def begin(i, j, local):
                k, s, g, c = quad_of(i, j), j % 2, (j // GROUP) % 2, (j % GROUP) * QUAD
                group = group_of(i, j)
                if j % GROUP == 0:
                    dve.wait_ge(msg_done, after(k - 3))
                    if not local:
                        nc.vector.tensor_copy(dst_i[:, g, :], dst_all[:, bass.ds(group * GT, GT)])
                    nc.vector.tensor_copy(cols[:, g, :], cols_all[:, bass.ds(group, 1), :].rearrange("p a c -> p (a c)")
                                          ).then_inc(cols_done, 1)
                dve.wait_ge(cols_done, after(group))
                dve.wait_ge(spread_done, after(k))
                if local:
                    dve.wait_ge(gather_done, after(k - 2))
                    nc.vector.tensor_scalar(onehot[:, s, :], dst_ps[:], cols[:, g, C_NODE:C_NODE + 1], None,
                                            ALU.is_equal).then_inc(onehot_done, 1)
                dve.wait_ge(sum_done, after(k - 2))
                for q in range(QUAD):
                    sl = slice(q * P, (q + 1) * P)
                    ins = nc.vector.scalar_tensor_tensor(out=merge[:, s, sl], in0=src_ps[:, sl],
                                                         scalar=cols[:, g, C_SRC + c + q:C_SRC + c + q + 1],
                                                         in1=tri[:], op0=ALU.is_equal, op1=ALU.mult,
                                                         accum_out=count[:, s, q:q + 1])
                ins.then_inc(merge_done, 1)

            def targets_a(i, j):
                k, s, g, c = quad_of(i, j), j % 2, (j // GROUP) % 2, (j % GROUP) * QUAD
                dve.wait_ge(merge_done, after(k))
                nc.vector.scalar_tensor_tensor(out=moved[:, s, :], in0=count[:, s, :], scalar=1.5,
                                               in1=cols[:, g, C_DUMMY + c:C_DUMMY + c + QUAD],
                                               op0=ALU.is_gt, op1=ALU.mult).then_inc(moved_done, 1)

            def targets_b(i, j):
                k, s, g, c = quad_of(i, j), j % 2, (j // GROUP) % 2, (j % GROUP) * QUAD
                dve.wait_ge(moved_done, after(k))
                dve.wait_ge(landed, after(k - 4) * QUAD)
                nc.vector.tensor_tensor(target[:, j % 4, :], moved[:, s, :], cols[:, g, C_SRC + c:C_SRC + c + QUAD],
                                        ALU.add).then_inc(target_done, 1)

            def softplus(i, j):
                k, s = quad_of(i, j), j % 2
                dve.wait_ge(log_done, after(k))
                dve.wait_ge(msg_done, after(k - 1))
                nc.vector.scalar_tensor_tensor(out=filt[:], in0=filt_ps[:, s, :], scalar=0.0, in1=logp[:, s, :],
                                               op0=ALU.max, op1=ALU.add).then_inc(filt_done, 1)

            def messages(i, j, local):
                k, s, g, c = quad_of(i, j), j % 2, (j // GROUP) % 2, (j % GROUP) * QUAD
                dve.wait_ge(filt_done, after(k))
                if local:
                    dve.wait_ge(gather_done, after(k))
                else:
                    dve.wait_ge(gathered[s], (i * 2 + j // 2 + 1) * (16 * QUAD))
                dve.wait_ge(sum_done, after(k - 2))
                rows_of_h = gath_ps if local else gath
                for q in range(QUAD):
                    sl = slice(q * P, (q + 1) * P)
                    ins = nc.vector.scalar_tensor_tensor(out=msg[:, s, sl], in0=filt[:, sl],
                                                         scalar=cols[:, g, C_WEIGHT + c + q:C_WEIGHT + c + q + 1],
                                                         in1=rows_of_h[:, s, sl], op0=ALU.mult, op1=ALU.mult)
                ins.then_inc(msg_done, 1)

            def step(i, j, local, last=False):
                more = not beyond(j + 1, last)
                if more:
                    begin(i, j + 1, local)
                if j >= 0:
                    softplus(i, j)
                if more:
                    targets_a(i, j + 1)
                if j >= 0:
                    messages(i, j, local)
                if more:
                    targets_b(i, j + 1)

            both_ways(dve, lambda local: steps(dve, step, local, head=(-1,)))

        @block.scalar
        def _(act):
            for s in (size_done, exp_done, log_done, stage_done):
                act.sem_inc(s, CREDIT)

            def chain(i, j):
                k, s = quad_of(i, j), j % 2
                act.wait_ge(linear_done, after(k))
                act.wait_ge(exp_done, after(k - 2))
                nc.scalar.activation(size[:, s, :], filt_ps[:, s, :], ACT.Abs).then_inc(size_done, 1)
                act.wait_ge(size_done, after(k))
                act.wait_ge(log_done, after(k - 2))
                nc.scalar.activation(expo[:, s, :], size[:, s, :], ACT.Exp, scale=-1.0).then_inc(exp_done, 1)
                act.wait_ge(exp_done, after(k))
                act.wait_ge(filt_done, after(k - 2))
                nc.scalar.activation(logp[:, s, :], expo[:, s, :], ACT.Ln, bias=S["half"][:, 0:1],
                                     scale=0.5).then_inc(log_done, 1)

            def stage_sums(i, j):
                k = quad_of(i, j)
                act.wait_ge(sum_done, after(k))
                act.wait_ge(landed, after(k - 4) * QUAD)
                nc.scalar.copy(stage[:, j % 4, :], sum_ps[:, j % 2, :]).then_inc(stage_done, 1)

            def step(i, j, local, last=False):
                if not beyond(j + 1, last):
                    chain(i, j + 1)
                if j >= 0:
                    stage_sums(i, j)

            nc.scalar.preload_act_table_set("natural_log_exp_and_others")
            both_ways(act, lambda local: steps(act, step, local, head=(-1,)))

        @block.gpsimd
        def _(pool):
            pool.sem_inc(landed, CREDIT * QUAD)

            def gather_rows(i, j):
                k, s, g, c = quad_of(i, j), j % 2, (j // GROUP) % 2, (j % GROUP) * QUAD
                pool.wait_ge(cols_done, after(group_of(i, j)))
                pool.wait_ge(msg_done, after(k - 2))
                pool.sem_inc(rows_asked, 1)
                for q in range(QUAD):
                    nc.gpsimd.indirect_dma_start(
                        gath[:, s, q * P:(q + 1) * P], None, A_["h"],
                        bass.IndirectOffsetOnAxis(ap=dst_i[:, g, c + q:c + q + 1], axis=0)).then_inc(gathered[s], 16)

            def add(i, j, first):
                k = quad_of(i, j)
                pool.wait_ge(target_done, after(k))
                pool.wait_ge(stage_done, after(k))
                for q in range(QUAD):
                    if not first:
                        pool.wait_ge(scattered[q], k * 16)
                        pool.sem_inc(landed, 1)
                    nc.gpsimd.indirect_dma_start(
                        A_["agg"][q], bass.IndirectOffsetOnAxis(ap=target[:, j % 4, q:q + 1], axis=0),
                        stage[:, j % 4, q * P:(q + 1) * P], None, compute_op=ALU.add).then_inc(scattered[q], 16)

            def step(i, j, local, last=False, first=False):
                if not local and not beyond(j + 1, last):
                    gather_rows(i, j + 1)
                add(i, j, first)

            def body(local):
                if not local:
                    gather_rows(0, 0)
                for j in range(4):
                    step(0, j, local, first=(j == 0))
                with pool.Fori(1, passes) as i:
                    for j in range(4):
                        step(i, j, local)
                for j in range(rest):
                    step(passes, j, local, last=True)
                for q in range(REPLICAS):
                    pool.wait_ge(scattered[q], 16 * quads)

            both_ways(pool, body)


def finish(nc, t):
    A_, S = t["dram"], t["sbuf"]
    ident = S["ident"]
    nodes = t["nodes"]
    nq = -(-nodes // QE)
    passes = (nq - 2) // 4
    rest = nq - 4 * passes
    tail = nodes - (nq - 1) * QE
    assert tail % QUAD == 0
    NIN = REPLICAS + 1

    with ExitStack() as ctx:
        def sb(name, shape, dt=F32):
            return ctx.enter_context(nc.sbuf_tensor(f"{name}_sb", shape, dt))

        def psum(name, shape):
            return ctx.enter_context(nc.psum_tensor(name, shape, F32))

        def sem(name):
            return ctx.enter_context(nc.semaphore(f"{name}_sem"))

        part_sum = sb("part_sum", [P, 4, REPLICAS, QE])
        x_in = sb("x_in", [P, 4, QE])
        pair_a = sb("pair_a", [P, 2, QE])
        pair_b = sb("pair_b", [P, 2, QE])
        aggT = sb("aggT", [P, 2, QE])
        size = sb("n_size", [P, 2, QE])
        expo = sb("n_expo", [P, 2, QE])
        logp = sb("n_logp", [P, 2, QE])
        soft = sb("soft", [P, QE])
        res = sb("res", [P, QE])
        stats = sb("stats", [P, QUAD, 6])
        moments = sb("moments", [P, 2, QUAD, 2])
        rstd = sb("rstd", [P, 2, QUAD])
        varep = sb("varep", [P, 2, QUAD])
        normed = sb("normed", [P, 4, QE])
        aggT_ps = psum("aggT_ps", [P, 2, QE])
        out_ps = psum("out_ps", [P, 2, QE])

        parts_in = [sem(f"parts_in{s}") for s in range(4)]
        stored = [sem(f"stored{s}") for s in range(4)]
        pair_a_done, pair_b_done = sem("pair_a_done"), sem("pair_b_done")
        turned, turned_sb, linear_done = sem("turned"), sem("turned_sb"), sem("n_linear_done")
        size_done, exp_done, log_done = sem("n_size_done"), sem("n_exp_done"), sem("n_log_done")
        soft_done, res_done, stats_done, moments_done = (sem("soft_done"), sem("res_done"), sem("stats_done"),
                                                         sem("moments_done"))
        varep_done, rstd_done, norm_done = sem("varep_done"), sem("rstd_done"), sem("norm_done")
        block = ctx.enter_context(nc.Block())

        def steps(eng, step, head=()):
            for j in head:
                step(0, j)
            with eng.Fori(0, passes) as i:
                for j in range(4):
                    step(i, j)
            for j in range(rest):
                step(passes, j, last=True)

        def beyond(j, last):
            return last and j >= rest

        @block.sync
        def _(sp):
            def step(i, j, last=False):
                k, s = quad_of(i, j), j % 4
                n = tail // QUAD if last and j == rest - 1 else P
                at = bass.ds(k * QE, n * QUAD)
                sp.wait_ge(pair_a_done, after(k - 4))
                sp.wait_ge(pair_b_done, after(k - 4))
                for r in range(REPLICAS):
                    sp.dma_start(part_sum[:, s, r, :], A_["agg"][r][bass.ds(k * QE, QE)].rearrange(
                        "(p t) f -> p (t f)", t=QUAD)).then_inc(parts_in[s], 16)
                sp.wait_ge(res_done, after(k - 4))
                sp.dma_start(x_in[0:n, s, :], A_["x"][at].rearrange("(p t) f -> p (t f)", t=QUAD)
                             ).then_inc(parts_in[s], 16)

            steps(sp, step)

        @block.gpsimd
        def _(pool):
            for s in (pair_b_done, rstd_done):
                pool.sem_inc(s, CREDIT)

            def add_pair(i, j):
                k, s = quad_of(i, j), j % 4
                pool.wait_ge(parts_in[s], (i + j // 4 + 1) * (16 * NIN))
                pool.wait_ge(turned, after(k - 2))
                nc.gpsimd.tensor_tensor(pair_b[:, j % 2, :], part_sum[:, s, 2, :], part_sum[:, s, 3, :],
                                        ALU.add).then_inc(pair_b_done, 1)

            def step(i, j, last=False):
                if not beyond(j + 2, last):
                    add_pair(i, j + 2)
                k = quad_of(i, j)
                pool.wait_ge(varep_done, after(k))
                nc.gpsimd.tensor_tensor(rstd[:, j % 2, :], varep[:, j % 2, :], S["minus_half"][:],
                                        ALU.pow).then_inc(rstd_done, 1)

            add_pair(0, 0)
            add_pair(0, 1)
            steps(pool, step)

        @block.tensor
        def _(pe):
            for s in (turned, linear_done):
                pe.sem_inc(s, CREDIT)

            def turn(i, j):
                k, s = quad_of(i, j), j % 2
                pe.wait_ge(pair_a_done, after(k))
                pe.wait_ge(pair_b_done, after(k))
                pe.wait_ge(turned_sb, after(k - 2))
                for q in range(QUAD):
                    sl = slice(q * P, (q + 1) * P)
                    nc.tensor.matmul(aggT_ps[:, s, sl], pair_a[:, s, sl], ident[:], start=True, stop=False)
                    mm = nc.tensor.matmul(aggT_ps[:, s, sl], pair_b[:, s, sl], ident[:], start=False, stop=True)
                mm.then_inc(turned, 1)

            def linear(i, j):
                k, s = quad_of(i, j), j % 2
                pe.wait_ge(turned_sb, after(k))
                pe.wait_ge(soft_done, after(k - 2))
                for q in range(QUAD):
                    sl = slice(q * P, (q + 1) * P)
                    nc.tensor.matmul(out_ps[:, s, sl], aggT[:, s, sl], S["w_out"][:], start=True, stop=False)
                    mm = nc.tensor.matmul(out_ps[:, s, sl], S["ones_row"][:], S["b_out"][:], start=False, stop=True)
                mm.then_inc(linear_done, 1)

            def step(i, j, last=False):
                if not beyond(j + 1, last):
                    turn(i, j + 1)
                if j >= 0:
                    linear(i, j)

            steps(pe, step, head=(-1,))

        @block.scalar
        def _(act):
            nc.scalar.preload_act_table_set("natural_log_exp_and_others")
            for s in (turned_sb, size_done, exp_done, log_done):
                act.sem_inc(s, CREDIT)

            def copy_turned(i, j):
                k, s = quad_of(i, j), j % 2
                act.wait_ge(turned, after(k))
                act.wait_ge(linear_done, after(k - 2))
                nc.scalar.copy(aggT[:, s, :], aggT_ps[:, s, :]).then_inc(turned_sb, 1)

            def chain(i, j):
                k, s = quad_of(i, j), j % 2
                act.wait_ge(linear_done, after(k))
                act.wait_ge(exp_done, after(k - 2))
                nc.scalar.activation(size[:, s, :], out_ps[:, s, :], ACT.Abs).then_inc(size_done, 1)
                act.wait_ge(size_done, after(k))
                act.wait_ge(log_done, after(k - 2))
                nc.scalar.activation(expo[:, s, :], size[:, s, :], ACT.Exp, scale=-1.0).then_inc(exp_done, 1)
                act.wait_ge(exp_done, after(k))
                act.wait_ge(soft_done, after(k - 2))
                nc.scalar.activation(logp[:, s, :], expo[:, s, :], ACT.Ln, bias=S["half"][:, 0:1],
                                     scale=0.5).then_inc(log_done, 1)

            def store(i, j, last=False):
                k, s = quad_of(i, j), j % 4
                n = tail // QUAD if last and j == rest - 1 else P
                act.wait_ge(norm_done, after(k))
                act.dma_start(A_["out"][bass.ds(k * QE, n * QUAD)].rearrange("(p t) f -> p (t f)", t=QUAD),
                              normed[0:n, s, :]).then_inc(stored[s], 16)

            def step(i, j, last=False):
                if not beyond(j + 1, last):
                    copy_turned(i, j + 1)
                if j >= 0:
                    chain(i, j)
                    store(i, j, last)

            steps(act, step, head=(-1,))
            for s in range(4):
                act.wait_ge(stored[s], 16 * -(-(nq - s) // 4))

        @block.vector
        def _(dve):
            for s in (pair_a_done, soft_done, res_done, stats_done, moments_done, varep_done, norm_done):
                dve.sem_inc(s, CREDIT)

            def add_pair(i, j):
                k, s = quad_of(i, j), j % 4
                dve.wait_ge(parts_in[s], (i + j // 4 + 1) * (16 * NIN))
                dve.wait_ge(turned, after(k - 2))
                nc.vector.tensor_tensor(pair_a[:, j % 2, :], part_sum[:, s, 0, :], part_sum[:, s, 1, :],
                                        ALU.add).then_inc(pair_a_done, 1)

            def normalise(i, j, again, add_next):
                k, s = quad_of(i, j), j % 2
                dve.wait_ge(log_done, after(k))
                dve.wait_ge(res_done, after(k - 1))
                nc.vector.scalar_tensor_tensor(out=soft[:], in0=out_ps[:, s, :], scalar=0.0, in1=logp[:, s, :],
                                               op0=ALU.max, op1=ALU.add).then_inc(soft_done, 1)
                dve.wait_ge(soft_done, after(k))
                dve.wait_ge(norm_done, after(k - 1))
                nc.vector.tensor_tensor(res[:], soft[:], x_in[:, j % 4, :], ALU.add).then_inc(res_done, 1)
                dve.wait_ge(res_done, after(k))
                for q in range(QUAD):
                    ins = nc.vector.bn_stats(stats[:, q, :], res[:, q * P:(q + 1) * P])
                ins.then_inc(stats_done, 1)
                dve.wait_ge(stats_done, after(k))
                if add_next:
                    add_pair(i, j + 2)
                for q in range(QUAD):
                    ins = nc.vector.bn_aggr(moments[:, s, q, :], stats[:, q, :])
                ins.then_inc(moments_done, 1)
                dve.wait_ge(moments_done, after(k))
                nc.vector.tensor_scalar(varep[:, s, :], moments[:, s, :, 1], EPS, None, ALU.add).then_inc(varep_done, 1)
                dve.wait_ge(rstd_done, after(k))
                if again:
                    dve.wait_ge(stored[j % 4], (i + j // 4) * 16)
                for q in range(QUAD):
                    sl = slice(q * P, (q + 1) * P)
                    ins = nc.vector.tensor_scalar(normed[:, j % 4, sl], res[:, sl], moments[:, s, q, 0:1],
                                                  rstd[:, s, q:q + 1], ALU.subtract, ALU.mult)
                ins.then_inc(norm_done, 1)

            def step(i, j, last=False, again=True):
                normalise(i, j, again, add_next=not beyond(j + 2, last))

            add_pair(0, 0)
            add_pair(0, 1)
            for j in range(4):
                step(0, j, again=False)
            with dve.Fori(1, passes) as i:
                for j in range(4):
                    step(i, j)
            for j in range(rest):
                step(passes, j, last=True)


def schnet_block(nc, xT, x, dst_g, src_nat, dst_nat, src_col, dst_col, w_col, attrT, w_inT, b_in, w_fT, b_f, w_outT,
                 b_out, out):
    nodes = x.shape[0]
    groups = dst_g.shape[0]
    edges_pad = groups * GE
    nodes_pad = xT.shape[1]
    KA = QUAD * w_fT.shape[0] + 1
    assert nodes_pad >= nodes + P
    with ExitStack() as ctx:
        def sb(name, shape, dt=F32):
            return ctx.enter_context(nc.sbuf_tensor(f"{name}_sb", shape, dt))

        dram = dict(xT=xT, x=x, dst_g=dst_g, src_nat=src_nat, dst_nat=dst_nat, src_col=src_col, dst_col=dst_col,
                    w_col=w_col, attrT=attrT, w_inT=w_inT, b_in=b_in, w_fT=w_fT, b_f=b_f, w_outT=w_outT, b_out=b_out, out=out)
        dram["h"] = nc.dram_tensor("h", (nodes_pad, P), F32, kind="Internal").ap()
        dram["rows"] = nc.dram_tensor("index_rows", (4, edges_pad), BF16, kind="Internal").ap()
        dram["bases"] = nc.dram_tensor("bases", (-(-groups // P) * P, 1), I32, kind="Internal").ap()
        dram["agg"] = [nc.dram_tensor(f"agg{r}", (nodes_pad, P), F32, kind="Internal").ap() for r in range(REPLICAS)]
        sbuf = dict(
            cols_all=sb("cols_all", [P, groups, COLS]),
            dst_all=sb("dst_all", [P, groups * GT], I32),
            attr=sb("attr", [KA, 2, GROUP * P]),
            ident=sb("ident", [P, P]),
            tri=sb("tri", [P, P]),
            w_f=sb("w_f", [KA, QE]),
            w_out=sb("w_out", [P, P]),
            b_out=sb("b_out", [1, P]),
            ones_row=sb("ones_row", [1, P]),
            half=sb("half", [P, 1]),
            minus_half=sb("minus_half", [P, QUAD]),
            sel_src=sb("sel_src", [4, P], BF16),
            sel_dst=sb("sel_dst", [4, P], BF16),
            base_row=sb("base_row", [1, groups], I32),
            flag=sb("flag", [1, 1], I32),
        )
        t = dict(dram=dram, sbuf=sbuf, nodes=nodes, nodes_pad=nodes_pad, groups=groups, tiles=groups * GT)
        prepare(nc, t)
        edges(nc, t)
        finish(nc, t)


def layouts(x, src, dst, edge_attr_20, edge_weight, L0_gnn_W_in, L0_gnn_b_in, L0_gnn_W_f, L0_gnn_b_f, L0_gnn_W_out,
            L0_gnn_b_out):
    import numpy as np
    nodes, E = x.shape[0], src.shape[0]
    groups = -(-E // GE)
    pad = groups * GE - E
    nodes_pad = -(-(nodes + P) // (HS * QE)) * (HS * QE)
    src = np.pad(np.asarray(src), (0, pad), mode="edge")
    dst = np.pad(np.asarray(dst), (0, pad), mode="edge")
    w = np.pad(np.asarray(edge_weight), (0, pad))
    attr = np.pad(np.asarray(edge_attr_20), ((0, pad), (0, 0)))
    c = np.ascontiguousarray
    return {
        "xT": c(np.pad(np.asarray(x), ((0, nodes_pad - nodes), (0, 0))).T),
        "x": c(x),
        "dst_g": c(dst.reshape(groups, GE)),
        "src_nat": c(src.reshape(P, -1)),
        "dst_nat": c(dst.reshape(P, -1)),
        "src_col": c(src.reshape(-1, P).T),
        "dst_col": c(dst.reshape(-1, P).T),
        "w_col": c(w.reshape(-1, P).T),
        "attrT": c(attr.reshape(groups * GROUP, QUAD, P, -1).transpose(1, 3, 0, 2).reshape(-1, groups * GROUP * P)),
        "w_inT": c(np.asarray(L0_gnn_W_in).T),
        "b_in": c(np.tile(np.asarray(L0_gnn_b_in)[None, :], (P, 1))),
        "w_fT": c(np.asarray(L0_gnn_W_f).T),
        "b_f": c(np.asarray(L0_gnn_b_f)[None, :]),
        "w_outT": c(np.asarray(L0_gnn_W_out).T),
        "b_out": c(np.asarray(L0_gnn_b_out)[None, :]),
    }


def kernel(**inputs):
    import concourse.bacc as _bacc
    from concourse.bass_utils import run_bass_kernel_spmd as _run

    nc = _bacc.Bacc("TRN2", target_bir_lowering=False, num_devices=1)
    arrays = {f"in_{n}": a for n, a in layouts(**inputs).items()}
    args = [nc.dram_tensor(n, a.shape, mybir.dt.from_np(a.dtype), kind="ExternalInput").ap() for n, a in arrays.items()]
    out = nc.dram_tensor("out", inputs["x"].shape, F32, kind="ExternalOutput").ap()
    schnet_block(nc, *args, out)
    return _run(nc, [arrays], core_ids=[0]).results[0]["out"]
```

```python
from contextlib import ExitStack

import concourse.bass as bass
from concourse import mybir

ALU = mybir.AluOpType
ACT = mybir.ActivationFunctionType
AX_X = mybir.AxisListType.X
F32 = mybir.dt.float32
BF16 = mybir.dt.bfloat16
I32 = mybir.dt.int32

P = 128
QUAD = 4
QE = QUAD * P
GROUP = 2
GT = GROUP * QUAD
GE = GROUP * QE
REPLICAS = QUAD
EPS = 1e-5
C_SRC, C_WEIGHT, C_DUMMY, C_NODE = 0, GT, 2 * GT, 3 * GT
COLS = 3 * GT + 1
CREDIT = 4
HS = 5


def after(k):
    return k + CREDIT + 1


def quad_of(i, j):
    return i * (2 * GROUP) + j


def group_of(i, j):
    return i * 2 + j // GROUP


def prepare(nc, t):
    A_, S = t["dram"], t["sbuf"]
    cols_all, ident, tri = S["cols_all"], S["ident"], S["tri"]
    nodes_pad, tiles, groups = t["nodes_pad"], t["tiles"], t["groups"]
    blocks = -(-groups // P)
    hi_mask = (-(-t["nodes"] // P) * P - 1)
    hi_mask = (1 << hi_mask.bit_length()) - P
    nq = nodes_pad // QE
    passes = nq // HS
    NA = A_["w_fT"].shape[0]
    assert nq % HS == 0 and hi_mask < (1 << 15)

    with ExitStack() as ctx:
        def sb(name, shape, dt):
            return ctx.enter_context(nc.sbuf_tensor(f"{name}_sb", shape, dt))

        def sem(name):
            return ctx.enter_context(nc.semaphore(f"{name}_sem"))

        src_nat = sb("src_nat", [P, tiles], I32)
        src_hi_int = sb("src_hi_int", [P, tiles], I32)
        src_hi = sb("src_hi", [P, tiles], BF16)
        src_lo = sb("src_lo", [P, tiles], BF16)
        dst_hi_int = sb("dst_hi_int", [P, GE], I32)
        dst_hi = sb("dst_hi", [P, blocks, GE], BF16)
        dst_lo = sb("dst_lo", [P, blocks, GE], BF16)
        src_col = sb("src_col", [P, tiles], I32)
        w_col = sb("w_col", [P, tiles], F32)
        dst_g = sb("dst_g", [P, blocks, GE], I32)
        least = sb("least", [P, blocks], F32)
        most = sb("most", [P, blocks], F32)
        span = sb("span", [P, blocks], F32)
        wide = sb("wide", [P, blocks], F32)
        wide_any = sb("wide_any", [P, 1], F32)
        base_int = sb("base_int", [P, blocks], I32)
        base_bc = sb("base_bc", [P, groups], I32)
        part_i = sb("part_i", [P, 1], I32)
        part = sb("part", [P, 1], F32)
        dummy = sb("dummy_row", [P, 1], F32)
        ones_col = sb("ones_col", [P, 1], F32)
        ones_sq = sb("ones_sq", [P, P], F32)
        zeros, zeroed = S["zeros"], t["zeroed"]
        xT = sb("xT", [P, HS, QE], F32)
        h_sb = sb("h_sb", [P, HS, QE], F32)
        w_in = sb("w_in", [P, P], F32)
        b_in = sb("b_in", [P, P], F32)
        h_ps = ctx.enter_context(nc.psum_tensor("h_ps", [P, HS, QE], F32))
        flag_ps = ctx.enter_context(nc.psum_tensor("flag_ps", [P, QE], F32))

        dstg_in, nat_in = sem("dstg_in"), sem("nat_in")
        col_in, w_in_sem, wts_in, tab_in = sem("col_in"), sem("w_in_sem"), sem("wts_in"), sem("tab_in")
        xT_in = [sem(f"xT_in{s}") for s in range(HS)]
        h_out = [sem(f"h_out{s}") for s in range(HS)]
        rows_out, base_out, base_in, basebc_in = (sem("rows_out"), sem("base_out"), sem("base_in"),
                                                  sem("basebc_in"))
        zeros_set, part_set, dummy_set = sem("zeros_set"), sem("part_set"), sem("dummy_set")
        lims_set, lims_done, span_done = (sem("lims_set"), sem("lims_done"),
                                                      sem("span_done"))
        base_done, flag_mm, flag_done, hi_masked = sem("base_done"), sem("flag_mm"), sem("flag_done"), sem("hi_masked")
        hi_done, lo_done, cols_set, h_mm, h_done = (sem("hi_done"), sem("lo_done"), sem("cols_set"), sem("h_mm"),
                                                    sem("h_done"))
        iota_done, sel_zero, sel_set = (sem("iota_done"), sem("sel_zero"),
                                                   sem("sel_set"))
        wf_zero, wf_in = sem("wf_zero"), sem("wf_in")
        masks_base, masks_done, weights_set = sem("masks_base"), sem("masks_done"), sem("weights_set")

        zeros_again = zeros[:].rearrange("p (a f) -> p a f", a=1).broadcast_to([P, 8, nodes_pad // 8])

        def agg_flat(r):
            return A_["agg"][r].rearrange("(p a) f -> p (a f)", p=P).rearrange("p (b c) -> p b c", b=8)

        block = ctx.enter_context(nc.Block())

        @block.sync
        def _(sp):
            for b in range(blocks):
                n = min(P, groups - b * P)
                sp.dma_start(dst_g[0:n, b, :], A_["dst_g"][b * P:b * P + n]).then_inc(dstg_in, 16)
            sp.dma_start(src_nat[:], A_["src_nat"]).then_inc(nat_in, 16)
            sp.dma_start(w_in[:], A_["w_inT"]).then_inc(wts_in, 16)
            sp.dma_start(b_in[:], A_["b_in"]).then_inc(wts_in, 16)
            def load_x(i, s, again):
                if again:
                    sp.wait_ge(h_mm, i * HS + (s + 1 - HS))
                sp.dma_start(xT[:, s, :], A_["xT"][:, bass.ds(i * (HS * QE) + s * QE, QE)]).then_inc(xT_in[s], 16)

            for s in range(HS):
                load_x(0, s, False)
            sp.dma_start(src_col[:], A_["src_col"]).then_inc(col_in, 16)
            sp.dma_start(w_col[:], A_["w_col"]).then_inc(w_in_sem, 16)
            sp.wait_ge(base_done, 1)
            for b in range(blocks):
                n = min(P, groups - b * P)
                sp.dma_start(A_["bases"][b * P:b * P + n], base_int[0:n, b:b + 1]).then_inc(base_out, 16)
            with sp.Fori(1, passes) as i:
                for s in range(HS):
                    load_x(i, s, True)
            sp.wait_ge(base_out, 16 * blocks)
            bases_row = A_["bases"].rearrange("g a -> a g")
            sp.dma_start(S["base_row"][:], bases_row[:, 0:groups]).then_inc(base_in, 16)
            sp.dma_start(base_bc[:], bases_row[:, 0:groups].broadcast_to([P, groups])).then_inc(basebc_in, 16)
            sp.wait_ge(wf_zero, 1)
            for q in range(QUAD):
                sl = slice(q * P, (q + 1) * P)
                sp.dma_start(S["w_f"][q * NA:(q + 1) * NA, sl], A_["w_fT"]).then_inc(wf_in, 16)
                sp.dma_start(S["w_f"][QUAD * NA:QUAD * NA + 1, sl], A_["b_f"]).then_inc(wf_in, 16)
            sp.dma_start(S["w_out"][:], A_["w_outT"]).then_inc(tab_in, 16)
            sp.dma_start(S["b_out"][:], A_["b_out"]).then_inc(tab_in, 16)
            sp.wait_ge(base_in, 16)
            sp.wait_ge(tab_in, 32)
            sp.wait_ge(wf_in, 32 * QUAD)

        @block.gpsimd
        def _(pool):
            nc.gpsimd.memset(zeros[:], 0.0).then_inc(zeros_set, 1)
            nc.gpsimd.iota(part_i[:], pattern=[[0, 1]], base=0, channel_multiplier=1).then_inc(iota_done, 1)
            nc.gpsimd.memset(ones_sq[:], 1.0).then_inc(masks_base, 1)
            pool.wait_ge(zeros_set, 1)
            for r in range(REPLICAS // 2):
                pool.dma_start(agg_flat(r), zeros_again).then_inc(zeroed[0], 16)
            pool.wait_ge(masks_base, 1)
            nc.gpsimd.affine_select(out=tri[:], in_=ones_sq[:], compare_op=ALU.is_ge, fill=0.0, base=0,
                                    pattern=[[-1, P]], channel_multiplier=1).then_inc(masks_done, 1)
            nc.gpsimd.affine_select(out=ident[:], in_=ones_sq[:], compare_op=ALU.is_equal, fill=0.0, base=0,
                                    pattern=[[-1, P]], channel_multiplier=1).then_inc(masks_done, 1)
            pool.wait_ge(w_in_sem, 16)
            nc.gpsimd.tensor_copy(cols_all[:, :, C_WEIGHT:C_WEIGHT + GT],
                                  w_col[:].rearrange("p (g t) -> p g t", t=GT)).then_inc(weights_set, 1)
            pool.wait_ge(weights_set, 1)
            pool.wait_ge(masks_done, 2)

        @block.scalar
        def _(act):
            def store_rows(r, half):
                act.dma_start(A_["rows"][r].rearrange("(p c) -> p c", p=P), half[:]).then_inc(rows_out, 16)

            def store_blocks(r, half):
                by_group = A_["rows"][r].rearrange("(g e) -> g e", e=GE)
                for b in range(blocks):
                    n = min(P, groups - b * P)
                    act.dma_start(by_group[b * P:b * P + n], half[0:n, b, :]).then_inc(rows_out, 16)

            for b in range(blocks):
                n = min(P, groups - b * P)
                act.wait_ge(hi_masked, b + 1)
                nc.scalar.copy(dst_hi[0:n, b, :], dst_hi_int[0:n, :]).then_inc(hi_done, 1)
            act.wait_ge(hi_masked, blocks + 1)
            nc.scalar.copy(src_hi[:], src_hi_int[:]).then_inc(hi_done, 1)
            act.wait_ge(hi_done, blocks + 1)
            act.wait_ge(lo_done, blocks + 1)
            store_rows(0, src_hi)
            store_rows(1, src_lo)
            store_blocks(2, dst_hi)
            store_blocks(3, dst_lo)

            def store_h(i, s):
                act.wait_ge(h_done, i * HS + (s + 1))
                rows = A_["h"][bass.ds(i * (HS * QE) + s * QE, QE)].rearrange("(p t) f -> p (t f)", t=QUAD)
                act.dma_start(rows, h_sb[:, s, :]).then_inc(h_out[s], 16)

            with act.Fori(0, passes) as i:
                for s in range(HS):
                    store_h(i, s)
            act.wait_ge(zeros_set, 1)
            for r in range(REPLICAS // 2, REPLICAS):
                act.dma_start(agg_flat(r), zeros_again).then_inc(zeroed[1], 16)
            for s in range(HS):
                act.wait_ge(h_out[s], 16 * passes)
            act.wait_ge(rows_out, 32 * (blocks + 1))

        @block.tensor
        def _(pe):
            pe.wait_ge(wts_in, 32)

            def products(i, s, again):
                pe.wait_ge(xT_in[s], i * 16 + 16)
                if again:
                    pe.wait_ge(h_done, i * HS + (s + 1 - HS))
                x_s = xT[:, s, :].rearrange("k (p t) -> k p t", t=QUAD)
                for q in range(QUAD):
                    mm = nc.tensor.matmul(h_ps[:, s, q * P:(q + 1) * P], x_s[:, :, q], w_in[:], start=True, stop=True)
                mm.then_inc(h_mm, 1)

            for s in range(HS):
                products(0, s, False)
            with pe.Fori(1, passes) as i:
                for s in range(HS):
                    products(i, s, True)
            pe.wait_ge(span_done, 3)
            nc.tensor.matmul(flag_ps[0:1, 0:1], wide_any[:], ones_col[:], start=True, stop=True).then_inc(flag_mm, 1)

        @block.vector
        def _(dve):
            nc.vector.memset(S["w_f"][:], 0.0).then_inc(wf_zero, 1)
            nc.vector.memset(least[:], 0.0).then_inc(lims_set, 1)
            nc.vector.memset(most[:], 0.0).then_inc(lims_set, 1)
            nc.vector.memset(ones_col[:], 1.0)
            nc.vector.memset(S["ones_row"][:], 1.0)
            nc.vector.memset(S["half"][:], 0.5)
            nc.vector.memset(S["minus_half"][:], -0.5)
            nc.vector.memset(S["attr"][:], 1.0)
            nc.vector.memset(S["sel_src"][:], 0.0).then_inc(sel_zero, 1)
            nc.vector.memset(S["sel_dst"][:], 1.0).then_inc(sel_zero, 1)
            dve.wait_ge(sel_zero, 2)
            nc.vector.memset(S["sel_src"][0:2, :], 1.0)
            nc.vector.memset(S["sel_dst"][0:2, :], 0.0).then_inc(sel_set, 1)
            dve.wait_ge(dstg_in, 16 * blocks)
            dve.wait_ge(lims_set, 2)
            for b in range(blocks):
                n = min(P, groups - b * P)
                nc.vector.tensor_reduce(least[0:n, b:b + 1], dst_g[0:n, b, :], AX_X, ALU.min).then_inc(lims_done, 1)
                nc.vector.tensor_reduce(most[0:n, b:b + 1], dst_g[0:n, b, :], AX_X, ALU.max).then_inc(lims_done, 1)
            dve.wait_ge(lims_done, 2 * blocks)
            nc.vector.tensor_copy(base_int[:], least[:]).then_inc(base_done, 1)
            nc.vector.tensor_tensor(span[:], most[:], least[:], ALU.subtract).then_inc(span_done, 1)
            dve.wait_ge(span_done, 1)
            nc.vector.tensor_scalar(wide[:], span[:], float(P - 1), None, ALU.is_gt).then_inc(span_done, 1)
            dve.wait_ge(span_done, 2)
            nc.vector.tensor_reduce(wide_any[:], wide[:], AX_X, ALU.add).then_inc(span_done, 1)

            for b in range(blocks):
                n = min(P, groups - b * P)
                if b:
                    dve.wait_ge(hi_done, b)
                    dve.wait_ge(lo_done, b)
                nc.vector.tensor_scalar(dst_hi_int[0:n, :], dst_g[0:n, b, :], hi_mask, None,
                                        ALU.bitwise_and).then_inc(hi_masked, 1)
                dve.wait_ge(hi_masked, b + 1)
                nc.vector.tensor_tensor(dst_lo[0:n, b, :], dst_g[0:n, b, :], dst_hi_int[0:n, :],
                                        ALU.subtract).then_inc(lo_done, 1)
            dve.wait_ge(nat_in, 16)
            nc.vector.tensor_scalar(src_hi_int[:], src_nat[:], hi_mask, None, ALU.bitwise_and).then_inc(hi_masked, 1)
            dve.wait_ge(hi_masked, blocks + 1)
            nc.vector.tensor_tensor(src_lo[:], src_nat[:], src_hi_int[:], ALU.subtract).then_inc(lo_done, 1)

            dve.wait_ge(iota_done, 1)
            nc.vector.tensor_copy(part[:], part_i[:]).then_inc(part_set, 1)
            dve.wait_ge(part_set, 1)
            nc.vector.tensor_scalar(dummy[:], part[:], float(t["nodes"]), None, ALU.add).then_inc(dummy_set, 1)

            def add_bias(i, s, again):
                dve.wait_ge(h_mm, i * HS + (s + 1))
                if again:
                    dve.wait_ge(h_out[s], i * 16)
                nc.vector.tensor_tensor(h_sb[:, s, :].rearrange("p (t f) -> p t f", t=QUAD),
                                        h_ps[:, s, :].rearrange("p (t f) -> p t f", t=QUAD),
                                        b_in[:].rearrange("p (a f) -> p a f", a=1).broadcast_to([P, QUAD, P]),
                                        ALU.add).then_inc(h_done, 1)

            dve.wait_ge(wts_in, 32)
            for s in range(HS):
                add_bias(0, s, False)
            with dve.Fori(1, passes) as i:
                for s in range(HS):
                    add_bias(i, s, True)

            dve.wait_ge(col_in, 16)
            nc.vector.tensor_copy(cols_all[:, :, C_SRC:C_SRC + GT],
                                  src_col[:].rearrange("p (g t) -> p g t", t=GT)).then_inc(cols_set, 1)
            dve.wait_ge(dummy_set, 1)
            nc.vector.tensor_scalar(cols_all[:, :, C_DUMMY:C_DUMMY + GT],
                                    src_col[:].rearrange("p (g t) -> p g t", t=GT), -1.0, dummy[:, 0:1],
                                    ALU.mult, ALU.add).then_inc(cols_set, 1)
            dve.wait_ge(flag_mm, 1)
            nc.vector.tensor_copy(S["flag"][:], flag_ps[0:1, 0:1]).then_inc(flag_done, 1)
            dve.wait_ge(basebc_in, 16)
            nc.vector.tensor_scalar(cols_all[:, :, C_NODE], base_bc[:], part[:, 0:1], None,
                                    ALU.add).then_inc(cols_set, 1)
            dve.wait_ge(cols_set, 3)
            dve.wait_ge(flag_done, 1)
            dve.wait_ge(sel_set, 1)


def edges(nc, t):
    A_, S = t["dram"], t["sbuf"]
    cols_all, dst_all, ident, tri = S["cols_all"], S["dst_all"], S["ident"], S["tri"]
    groups = t["groups"]
    quads = groups * GROUP
    passes = (groups - 1) // 2
    rest = quads - 4 * passes

    with ExitStack() as ctx:
        def sb(name, shape, dt):
            return ctx.enter_context(nc.sbuf_tensor(f"{name}_sb", shape, dt))

        def psum(name, shape):
            return ctx.enter_context(nc.psum_tensor(name, shape, F32))

        def sem(name):
            return ctx.enter_context(nc.semaphore(f"{name}_sem"))

        attr = S["attr"]
        KA = attr.shape[0]
        rows = sb("rows", [4, 2, GE], BF16)
        window = sb("window", [P, 2, P], F32)
        cols = sb("cols", [P, 2, COLS], F32)
        dst_i = sb("dst_i", [P, 2, GT], I32)
        onehot = sb("onehot", [P, 2, QE], F32)
        merge = sb("merge", [P, 4, QE], F32)
        count = sb("count", [P, 2, QUAD], F32)
        moved = sb("moved", [P, 2, QUAD], F32)
        target = sb("target", [P, 4, QUAD], I32)
        size = sb("size", [P, 2, QE], F32)
        expo = sb("expo", [P, 2, QE], F32)
        logp = sb("logp", [P, 2, QE], F32)
        filt = sb("filt", [P, QE], F32)
        gath = sb("gath", [P, 2, QE], F32)
        msg = sb("msg", [P, 2, QE], F32)
        stage = sb("stage", [P, 4, QE], F32)
        src_ps = psum("src_ps", [P, QE])
        dst_ps = psum("dst_ps", [P, QE])
        filt_ps = psum("filt_ps", [P, 2, QE])
        gath_ps = psum("gath_ps", [P, 2, QE])
        sum_ps = psum("sum_ps", [P, 2, QE])

        dst_all_in = sem("dst_all_in")
        loads_in = [sem(f"loads_in{s}") for s in range(2)]
        gathered = [sem(f"gathered{s}") for s in range(2)]
        scattered = [sem(f"scattered{r}") for r in range(REPLICAS)]
        spread_done = sem("spread_done")
        onehot_done = sem("onehot_done")
        merge_done = sem("merge_done")
        target_done = sem("target_done")
        gather_done = sem("gather_done")
        linear_done = sem("linear_done")
        size_done, exp_done, log_done = sem("size_done"), sem("exp_done"), sem("log_done")
        filt_done = sem("filt_done")
        msg_done = sem("msg_done")
        sum_done = sem("sum_done")
        stage_done = sem("stage_done")
        landed = sem("landed")
        rows_asked = sem("rows_asked")
        moved_done = sem("moved_done")
        cols_done = sem("cols_done")

        block = ctx.enter_context(nc.Block())

        def both_ways(eng, body):
            wide = eng.value_load(S["flag"][0:1, 0:1], min_val=0, max_val=groups)
            with eng.If(wide == 0):
                body(True)
            with eng.Else():
                body(False)

        def steps(eng, step, local, head=()):
            for j in head:
                step(0, j, local)
            with eng.Fori(0, passes) as i:
                for j in range(4):
                    step(i, j, local)
            for j in range(rest):
                step(passes, j, local, last=True)

        def beyond(j, last):
            return last and j >= rest

        @block.sync
        def _(sp):
            def load(i, g, local):
                s = g % 2
                group = i * 2 + g
                sp.wait_ge(linear_done, after((group - 2) * GROUP + 1))
                sp.wait_ge(spread_done, after((group - 2) * GROUP + 1))
                sp.dma_start(attr[0:KA - 1, s, :], A_["attrT"][:, bass.ds(group * (GROUP * P), GROUP * P)]
                             ).then_inc(loads_in[s], 16)
                sp.dma_start(rows[:, s, :], A_["rows"][:, bass.ds(group * GE, GE)]).then_inc(loads_in[s], 16)
                if local:
                    sp.wait_ge(gather_done, after((group - 2) * GROUP + 1))
                    base = sp.value_load(S["base_row"][0:1, bass.ds(group, 1)], min_val=0, max_val=t["nodes"] - 1)
                    sp.dma_start(window[:, s, :], A_["h"][bass.ds(base, P)]).then_inc(loads_in[s], 16)

            def body(local):
                if not local:
                    sp.dma_start(dst_all[:], A_["dst_col"]).then_inc(dst_all_in, 16)
                with sp.Fori(0, passes) as i:
                    for g in range(2):
                        load(i, g, local)
                for g in range(rest // GROUP):
                    load(passes, g, local)

            both_ways(sp, body)

        def loads(local):
            return 48 if local else 32

        @block.tensor
        def _(pe):
            for s in (spread_done, gather_done, linear_done, sum_done):
                pe.sem_inc(s, CREDIT)

            def arrived(i, j, local):
                pe.wait_ge(loads_in[(j // GROUP) % 2], (i + (j // GROUP) // 2 + 1) * loads(local))

            def spread(i, j, local):
                k, g, e = quad_of(i, j), (j // GROUP) % 2, (j % GROUP) * QE
                arrived(i, j, local)
                pe.wait_ge(merge_done, after(k - 1))
                nc.tensor.matmul(src_ps[:], S["sel_src"][:], rows[:, g, e:e + QE], start=True, stop=True)
                if local:
                    pe.wait_ge(onehot_done, after(k - 1))
                mm = nc.tensor.matmul(dst_ps[:], S["sel_dst"][:], rows[:, g, e:e + QE], start=True, stop=True)
                mm.then_inc(spread_done, 1)

            def linear(i, j, local):
                k, g, e = quad_of(i, j), (j // GROUP) % 2, (j % GROUP) * P
                arrived(i, j, local)
                pe.wait_ge(filt_done, after(k - 2))
                mm = nc.tensor.matmul(filt_ps[:, j % 2, :], attr[:, g, e:e + P], S["w_f"][:], start=True, stop=True)
                mm.then_inc(linear_done, 1)

            def gather(i, j, local):
                k, g = quad_of(i, j), (j // GROUP) % 2
                pe.wait_ge(onehot_done, after(k))
                pe.wait_ge(msg_done, after(k - 2))
                for q in range(QUAD):
                    mm = nc.tensor.matmul(gath_ps[:, j % 2, q * P:(q + 1) * P], onehot[:, j % 2, q * P:(q + 1) * P],
                                          window[:, g, :], start=True, stop=True)
                mm.then_inc(gather_done, 1)

            def merge_sources(i, j):
                k = quad_of(i, j)
                pe.wait_ge(merge_done, after(k))
                pe.wait_ge(msg_done, after(k))
                pe.wait_ge(stage_done, after(k - 2))
                for q in range(QUAD):
                    sl = slice(q * P, (q + 1) * P)
                    mm = nc.tensor.matmul(sum_ps[:, j % 2, sl], merge[:, j % 4, sl], msg[:, j % 2, sl],
                                          start=True, stop=True)
                mm.then_inc(sum_done, 1)

            def step(i, j, local, last=False):
                if local and not beyond(j + 1, last):
                    gather(i, j + 1, local)
                if not beyond(j + 2, last):
                    spread(i, j + 2, local)
                    linear(i, j + 2, local)
                if j >= 0:
                    merge_sources(i, j)

            def body(local):
                spread(0, 0, local)
                linear(0, 0, local)
                steps(pe, step, local, head=(-1,))

            both_ways(pe, body)

        @block.vector
        def _(dve):
            for s in (onehot_done, merge_done, target_done, filt_done, msg_done, moved_done, cols_done):
                dve.sem_inc(s, CREDIT)

            def begin(i, j, local):
                k, s, g, c = quad_of(i, j), j % 2, (j // GROUP) % 2, (j % GROUP) * QUAD
                group = group_of(i, j)
                if j % GROUP == 0:
                    dve.wait_ge(msg_done, after(k - 3))
                    if not local:
                        nc.vector.tensor_copy(dst_i[:, g, :], dst_all[:, bass.ds(group * GT, GT)])
                    nc.vector.tensor_copy(cols[:, g, :], cols_all[:, bass.ds(group, 1), :].rearrange("p a c -> p (a c)")
                                          ).then_inc(cols_done, 1)
                dve.wait_ge(cols_done, after(group))
                dve.wait_ge(spread_done, after(k))
                if local:
                    dve.wait_ge(gather_done, after(k - 2))
                    nc.vector.tensor_scalar(onehot[:, s, :], dst_ps[:], cols[:, g, C_NODE:C_NODE + 1], None,
                                            ALU.is_equal).then_inc(onehot_done, 1)
                dve.wait_ge(sum_done, after(k - 4))
                for q in range(QUAD):
                    sl = slice(q * P, (q + 1) * P)
                    ins = nc.vector.scalar_tensor_tensor(out=merge[:, j % 4, sl], in0=src_ps[:, sl],
                                                         scalar=cols[:, g, C_SRC + c + q:C_SRC + c + q + 1],
                                                         in1=tri[:], op0=ALU.is_equal, op1=ALU.mult,
                                                         accum_out=count[:, s, q:q + 1])
                ins.then_inc(merge_done, 1)

            def targets_a(i, j):
                k, s, g, c = quad_of(i, j), j % 2, (j // GROUP) % 2, (j % GROUP) * QUAD
                dve.wait_ge(merge_done, after(k))
                nc.vector.scalar_tensor_tensor(out=moved[:, s, :], in0=count[:, s, :], scalar=1.5,
                                               in1=cols[:, g, C_DUMMY + c:C_DUMMY + c + QUAD],
                                               op0=ALU.is_gt, op1=ALU.mult).then_inc(moved_done, 1)

            def targets_b(i, j):
                k, s, g, c = quad_of(i, j), j % 2, (j // GROUP) % 2, (j % GROUP) * QUAD
                dve.wait_ge(moved_done, after(k))
                dve.wait_ge(landed, after(k - 4) * QUAD)
                nc.vector.tensor_tensor(target[:, j % 4, :], moved[:, s, :], cols[:, g, C_SRC + c:C_SRC + c + QUAD],
                                        ALU.add).then_inc(target_done, 1)

            def softplus(i, j):
                k, s = quad_of(i, j), j % 2
                dve.wait_ge(log_done, after(k))
                dve.wait_ge(msg_done, after(k - 1))
                nc.vector.scalar_tensor_tensor(out=filt[:], in0=filt_ps[:, s, :], scalar=0.0, in1=logp[:, s, :],
                                               op0=ALU.max, op1=ALU.add).then_inc(filt_done, 1)

            def messages(i, j, local):
                k, s, g, c = quad_of(i, j), j % 2, (j // GROUP) % 2, (j % GROUP) * QUAD
                dve.wait_ge(filt_done, after(k))
                if local:
                    dve.wait_ge(gather_done, after(k))
                else:
                    dve.wait_ge(gathered[s], (i * 2 + j // 2 + 1) * (16 * QUAD))
                dve.wait_ge(sum_done, after(k - 2))
                rows_of_h = gath_ps if local else gath
                for q in range(QUAD):
                    sl = slice(q * P, (q + 1) * P)
                    ins = nc.vector.scalar_tensor_tensor(out=msg[:, s, sl], in0=filt[:, sl],
                                                         scalar=cols[:, g, C_WEIGHT + c + q:C_WEIGHT + c + q + 1],
                                                         in1=rows_of_h[:, s, sl], op0=ALU.mult, op1=ALU.mult)
                ins.then_inc(msg_done, 1)

            def step(i, j, local, last=False):
                more = not beyond(j + 1, last)
                if more:
                    begin(i, j + 1, local)
                if j >= 0:
                    softplus(i, j)
                if more:
                    targets_a(i, j + 1)
                if j >= 0:
                    messages(i, j, local)
                if more:
                    targets_b(i, j + 1)

            def body(local):
                if not local:
                    dve.wait_ge(dst_all_in, 16)
                steps(dve, step, local, head=(-1,))

            both_ways(dve, body)

        @block.scalar
        def _(act):
            for s in (size_done, exp_done, log_done, stage_done):
                act.sem_inc(s, CREDIT)

            def chain(i, j):
                k, s = quad_of(i, j), j % 2
                act.wait_ge(linear_done, after(k))
                act.wait_ge(exp_done, after(k - 2))
                nc.scalar.activation(size[:, s, :], filt_ps[:, s, :], ACT.Abs).then_inc(size_done, 1)
                act.wait_ge(size_done, after(k))
                act.wait_ge(log_done, after(k - 2))
                nc.scalar.activation(expo[:, s, :], size[:, s, :], ACT.Exp, scale=-1.0).then_inc(exp_done, 1)
                act.wait_ge(exp_done, after(k))
                act.wait_ge(filt_done, after(k - 2))
                nc.scalar.activation(logp[:, s, :], expo[:, s, :], ACT.Ln, bias=S["half"][:, 0:1],
                                     scale=0.5).then_inc(log_done, 1)

            def stage_sums(i, j):
                k = quad_of(i, j)
                act.wait_ge(sum_done, after(k))
                act.wait_ge(landed, after(k - 4) * QUAD)
                nc.scalar.copy(stage[:, j % 4, :], sum_ps[:, j % 2, :]).then_inc(stage_done, 1)

            def step(i, j, local, last=False):
                if not beyond(j + 1, last):
                    chain(i, j + 1)
                if j >= 0:
                    stage_sums(i, j)

            nc.scalar.preload_act_table_set("natural_log_exp_and_others")
            both_ways(act, lambda local: steps(act, step, local, head=(-1,)))

        @block.gpsimd
        def _(pool):
            pool.sem_inc(landed, CREDIT * QUAD)

            def gather_rows(i, j):
                k, s, g, c = quad_of(i, j), j % 2, (j // GROUP) % 2, (j % GROUP) * QUAD
                pool.wait_ge(cols_done, after(group_of(i, j)))
                pool.wait_ge(msg_done, after(k - 2))
                pool.sem_inc(rows_asked, 1)
                for q in range(QUAD):
                    nc.gpsimd.indirect_dma_start(
                        gath[:, s, q * P:(q + 1) * P], None, A_["h"],
                        bass.IndirectOffsetOnAxis(ap=dst_i[:, g, c + q:c + q + 1], axis=0)).then_inc(gathered[s], 16)

            def add(i, j, first):
                k = quad_of(i, j)
                pool.wait_ge(target_done, after(k))
                pool.wait_ge(stage_done, after(k))
                for q in range(QUAD):
                    if not first:
                        pool.wait_ge(scattered[q], k * 16)
                        pool.sem_inc(landed, 1)
                    nc.gpsimd.indirect_dma_start(
                        A_["agg"][q], bass.IndirectOffsetOnAxis(ap=target[:, j % 4, q:q + 1], axis=0),
                        stage[:, j % 4, q * P:(q + 1) * P], None, compute_op=ALU.add).then_inc(scattered[q], 16)

            def step(i, j, local, last=False, first=False):
                if not local and not beyond(j + 1, last):
                    gather_rows(i, j + 1)
                add(i, j, first)

            def body(local):
                if not local:
                    gather_rows(0, 0)
                for half in t["zeroed"]:
                    pool.wait_ge(half, 16 * REPLICAS // 2)
                for j in range(4):
                    step(0, j, local, first=(j == 0))
                with pool.Fori(1, passes) as i:
                    for j in range(4):
                        step(i, j, local)
                for j in range(rest):
                    step(passes, j, local, last=True)
                for q in range(REPLICAS):
                    pool.wait_ge(scattered[q], 16 * quads)

            both_ways(pool, body)


def finish(nc, t):
    A_, S = t["dram"], t["sbuf"]
    ident = S["ident"]
    nodes = t["nodes"]
    nq = -(-nodes // QE)
    passes = (nq - 4) // 4
    rest = nq - 4 * passes
    tail = nodes - (nq - 1) * QE
    assert tail % QUAD == 0
    NIN = REPLICAS + 1

    with ExitStack() as ctx:
        def sb(name, shape, dt=F32):
            return ctx.enter_context(nc.sbuf_tensor(f"{name}_sb", shape, dt))

        def psum(name, shape):
            return ctx.enter_context(nc.psum_tensor(name, shape, F32))

        def sem(name):
            return ctx.enter_context(nc.semaphore(f"{name}_sem"))

        part_sum = sb("part_sum", [P, 4, REPLICAS, QE])
        x_in = sb("x_in", [P, 4, QE])
        pair_a = sb("pair_a", [P, 2, QE])
        pair_b = sb("pair_b", [P, 2, QE])
        aggT = sb("aggT", [P, 2, QE])
        size = sb("n_size", [P, 2, QE])
        expo = sb("n_expo", [P, 2, QE])
        logp = sb("n_logp", [P, 2, QE])
        soft = sb("soft", [P, QE])
        res = sb("res", [P, 2, QE])
        stats = sb("stats", [P, QUAD, 6])
        moments = sb("moments", [P, 2, QUAD, 2])
        rstd = sb("rstd", [P, 2, QUAD])
        varep = sb("varep", [P, 2, QUAD])
        normed = sb("normed", [P, 4, QE])
        aggT_ps = psum("aggT_ps", [P, 2, QE])
        out_ps = psum("out_ps", [P, 2, QE])

        parts_in = [sem(f"parts_in{s}") for s in range(4)]
        stored = [sem(f"stored{s}") for s in range(4)]
        pair_a_done, pair_b_done = sem("pair_a_done"), sem("pair_b_done")
        turned, turned_sb, linear_done = sem("turned"), sem("turned_sb"), sem("n_linear_done")
        size_done, exp_done, log_done = sem("n_size_done"), sem("n_exp_done"), sem("n_log_done")
        soft_done, res_done, stats_done, moments_done = (sem("soft_done"), sem("res_done"), sem("stats_done"),
                                                         sem("moments_done"))
        varep_done, rstd_done, norm_done = sem("varep_done"), sem("rstd_done"), sem("norm_done")
        block = ctx.enter_context(nc.Block())

        def steps(eng, step, head=()):
            for j in head:
                step(0, j)
            with eng.Fori(0, passes) as i:
                for j in range(4):
                    step(i, j)
            for j in range(rest):
                step(passes, j, last=True)

        def beyond(j, last):
            return last and j >= rest

        @block.sync
        def _(sp):
            def step(i, j, last=False):
                k, s = quad_of(i, j), j % 4
                n = tail // QUAD if last and j == rest - 1 else P
                at = bass.ds(k * QE, n * QUAD)
                sp.wait_ge(pair_a_done, after(k - 4))
                sp.wait_ge(pair_b_done, after(k - 4))
                for r in range(REPLICAS):
                    sp.dma_start(part_sum[:, s, r, :], A_["agg"][r][bass.ds(k * QE, QE)].rearrange(
                        "(p t) f -> p (t f)", t=QUAD)).then_inc(parts_in[s], 16)
                sp.wait_ge(res_done, after(k - 4))
                sp.dma_start(x_in[0:n, s, :], A_["x"][at].rearrange("(p t) f -> p (t f)", t=QUAD)
                             ).then_inc(parts_in[s], 16)

            steps(sp, step)

        @block.gpsimd
        def _(pool):
            for s in (pair_b_done, rstd_done):
                pool.sem_inc(s, CREDIT)

            def add_pair(i, j):
                k, s = quad_of(i, j), j % 4
                pool.wait_ge(parts_in[s], (i + j // 4 + 1) * (16 * NIN))
                pool.wait_ge(turned, after(k - 2))
                nc.gpsimd.tensor_tensor(pair_b[:, j % 2, :], part_sum[:, s, 2, :], part_sum[:, s, 3, :],
                                        ALU.add).then_inc(pair_b_done, 1)

            def step(i, j, last=False):
                if not beyond(j + 3, last):
                    add_pair(i, j + 3)
                k = quad_of(i, j)
                pool.wait_ge(varep_done, after(k))
                nc.gpsimd.tensor_tensor(rstd[:, j % 2, :], varep[:, j % 2, :], S["minus_half"][:],
                                        ALU.pow).then_inc(rstd_done, 1)

            for j in range(3):
                add_pair(0, j)
            steps(pool, step)

        @block.tensor
        def _(pe):
            for s in (turned, linear_done):
                pe.sem_inc(s, CREDIT)

            def turn(i, j):
                k, s = quad_of(i, j), j % 2
                pe.wait_ge(pair_a_done, after(k))
                pe.wait_ge(pair_b_done, after(k))
                pe.wait_ge(turned_sb, after(k - 2))
                for q in range(QUAD):
                    sl = slice(q * P, (q + 1) * P)
                    nc.tensor.matmul(aggT_ps[:, s, sl], pair_a[:, s, sl], ident[:], start=True, stop=False)
                    mm = nc.tensor.matmul(aggT_ps[:, s, sl], pair_b[:, s, sl], ident[:], start=False, stop=True)
                mm.then_inc(turned, 1)

            def linear(i, j):
                k, s = quad_of(i, j), j % 2
                pe.wait_ge(turned_sb, after(k))
                pe.wait_ge(soft_done, after(k - 2))
                for q in range(QUAD):
                    sl = slice(q * P, (q + 1) * P)
                    nc.tensor.matmul(out_ps[:, s, sl], aggT[:, s, sl], S["w_out"][:], start=True, stop=False)
                    mm = nc.tensor.matmul(out_ps[:, s, sl], S["ones_row"][:], S["b_out"][:], start=False, stop=True)
                mm.then_inc(linear_done, 1)

            def step(i, j, last=False):
                if not beyond(j + 2, last):
                    turn(i, j + 2)
                if j + 1 >= 0 and not beyond(j + 1, last):
                    linear(i, j + 1)

            steps(pe, step, head=(-2, -1))

        @block.scalar
        def _(act):
            nc.scalar.preload_act_table_set("natural_log_exp_and_others")
            for s in (turned_sb, size_done, exp_done, log_done):
                act.sem_inc(s, CREDIT)

            def copy_turned(i, j):
                k, s = quad_of(i, j), j % 2
                act.wait_ge(turned, after(k))
                act.wait_ge(linear_done, after(k - 2))
                nc.scalar.copy(aggT[:, s, :], aggT_ps[:, s, :]).then_inc(turned_sb, 1)

            def chain(i, j):
                k, s = quad_of(i, j), j % 2
                act.wait_ge(linear_done, after(k))
                act.wait_ge(exp_done, after(k - 2))
                nc.scalar.activation(size[:, s, :], out_ps[:, s, :], ACT.Abs).then_inc(size_done, 1)
                act.wait_ge(size_done, after(k))
                act.wait_ge(log_done, after(k - 2))
                nc.scalar.activation(expo[:, s, :], size[:, s, :], ACT.Exp, scale=-1.0).then_inc(exp_done, 1)
                act.wait_ge(exp_done, after(k))
                act.wait_ge(soft_done, after(k - 2))
                nc.scalar.activation(logp[:, s, :], expo[:, s, :], ACT.Ln, bias=S["half"][:, 0:1],
                                     scale=0.5).then_inc(log_done, 1)

            def store(i, j, last=False):
                k, s = quad_of(i, j), j % 4
                n = tail // QUAD if last and j == rest - 1 else P
                act.wait_ge(norm_done, after(k))
                act.dma_start(A_["out"][bass.ds(k * QE, n * QUAD)].rearrange("(p t) f -> p (t f)", t=QUAD),
                              normed[0:n, s, :]).then_inc(stored[s], 16)

            def step(i, j, last=False, stores=True):
                if not beyond(j + 2, last):
                    copy_turned(i, j + 2)
                if j + 1 >= 0 and not beyond(j + 1, last):
                    chain(i, j + 1)
                if stores:
                    store(i, j - 2, last)

            for j in range(-2, 4):
                step(0, j, stores=j >= 2)
            with act.Fori(1, passes) as i:
                for j in range(4):
                    step(i, j)
            for j in range(rest):
                step(passes, j, last=True)
            for j in (rest - 2, rest - 1):
                store(passes, j, last=True)
            for s in range(4):
                act.wait_ge(stored[s], 16 * -(-(nq - s) // 4))

        @block.vector
        def _(dve):
            for s in (pair_a_done, soft_done, res_done, stats_done, moments_done, varep_done, norm_done):
                dve.sem_inc(s, CREDIT)

            def add_pair(i, j):
                k, s = quad_of(i, j), j % 4
                dve.wait_ge(parts_in[s], (i + j // 4 + 1) * (16 * NIN))
                dve.wait_ge(turned, after(k - 2))
                nc.vector.tensor_tensor(pair_a[:, j % 2, :], part_sum[:, s, 0, :], part_sum[:, s, 1, :],
                                        ALU.add).then_inc(pair_a_done, 1)

            def residual(i, j, add_next):
                k, s = quad_of(i, j), j % 2
                dve.wait_ge(log_done, after(k))
                dve.wait_ge(res_done, after(k - 1))
                nc.vector.scalar_tensor_tensor(out=soft[:], in0=out_ps[:, s, :], scalar=0.0, in1=logp[:, s, :],
                                               op0=ALU.max, op1=ALU.add).then_inc(soft_done, 1)
                dve.wait_ge(soft_done, after(k))
                dve.wait_ge(norm_done, after(k - 2))
                nc.vector.tensor_tensor(res[:, s, :], soft[:], x_in[:, j % 4, :], ALU.add).then_inc(res_done, 1)
                dve.wait_ge(res_done, after(k))
                for q in range(QUAD):
                    ins = nc.vector.bn_stats(stats[:, q, :], res[:, s, q * P:(q + 1) * P])
                ins.then_inc(stats_done, 1)
                dve.wait_ge(stats_done, after(k))
                if add_next:
                    add_pair(i, j + 3)
                for q in range(QUAD):
                    ins = nc.vector.bn_aggr(moments[:, s, q, :], stats[:, q, :])
                ins.then_inc(moments_done, 1)
                dve.wait_ge(moments_done, after(k))
                nc.vector.tensor_scalar(varep[:, s, :], moments[:, s, :, 1], EPS, None, ALU.add).then_inc(varep_done, 1)

            def normalise(i, j, again):
                k, s = quad_of(i, j), j % 2
                dve.wait_ge(rstd_done, after(k))
                if again:
                    dve.wait_ge(stored[j % 4], (i + j // 4) * 16)
                for q in range(QUAD):
                    sl = slice(q * P, (q + 1) * P)
                    ins = nc.vector.tensor_scalar(normed[:, j % 4, sl], res[:, s, sl], moments[:, s, q, 0:1],
                                                  rstd[:, s, q:q + 1], ALU.subtract, ALU.mult)
                ins.then_inc(norm_done, 1)

            def step(i, j, last=False, again=True):
                if not beyond(j + 1, last):
                    residual(i, j + 1, add_next=not beyond(j + 4, last))
                normalise(i, j, again)

            for j in range(3):
                add_pair(0, j)
            residual(0, 0, add_next=True)
            for j in range(4):
                step(0, j, again=False)
            with dve.Fori(1, passes) as i:
                for j in range(4):
                    step(i, j)
            for j in range(rest):
                step(passes, j, last=True)


def schnet_block(nc, xT, x, dst_g, src_nat, src_col, dst_col, w_col, attrT, w_inT, b_in, w_fT, b_f, w_outT,
                 b_out, out):
    nodes = x.shape[0]
    groups = dst_g.shape[0]
    edges_pad = groups * GE
    nodes_pad = xT.shape[1]
    KA = QUAD * w_fT.shape[0] + 1
    assert nodes_pad >= nodes + P
    with ExitStack() as ctx:
        def sb(name, shape, dt=F32):
            return ctx.enter_context(nc.sbuf_tensor(f"{name}_sb", shape, dt))

        dram = dict(xT=xT, x=x, dst_g=dst_g, src_nat=src_nat, src_col=src_col, dst_col=dst_col,
                    w_col=w_col, attrT=attrT, w_inT=w_inT, b_in=b_in, w_fT=w_fT, b_f=b_f, w_outT=w_outT, b_out=b_out, out=out)
        zeroed = [ctx.enter_context(nc.semaphore(f"zeroed_{queue}_sem")) for queue in ("pool", "act")]
        dram["h"] = nc.dram_tensor("h", (nodes_pad, P), F32, kind="Internal").ap()
        dram["rows"] = nc.dram_tensor("index_rows", (4, edges_pad), BF16, kind="Internal").ap()
        dram["bases"] = nc.dram_tensor("bases", (-(-groups // P) * P, 1), I32, kind="Internal").ap()
        dram["agg"] = [nc.dram_tensor(f"agg{r}", (nodes_pad, P), F32, kind="Internal").ap() for r in range(REPLICAS)]
        sbuf = dict(
            cols_all=sb("cols_all", [P, groups, COLS]),
            dst_all=sb("dst_all", [P, groups * GT], I32),
            attr=sb("attr", [KA, 2, GROUP * P]),
            ident=sb("ident", [P, P]),
            tri=sb("tri", [P, P]),
            w_f=sb("w_f", [KA, QE]),
            w_out=sb("w_out", [P, P]),
            b_out=sb("b_out", [1, P]),
            ones_row=sb("ones_row", [1, P]),
            zeros=sb("zeros", [P, nodes_pad // 8]),
            half=sb("half", [P, 1]),
            minus_half=sb("minus_half", [P, QUAD]),
            sel_src=sb("sel_src", [4, P], BF16),
            sel_dst=sb("sel_dst", [4, P], BF16),
            base_row=sb("base_row", [1, groups], I32),
            flag=sb("flag", [1, 1], I32),
        )
        t = dict(dram=dram, sbuf=sbuf, nodes=nodes, nodes_pad=nodes_pad, groups=groups, tiles=groups * GT,
                 zeroed=zeroed)
        prepare(nc, t)
        edges(nc, t)
        finish(nc, t)


def layouts(x, src, dst, edge_attr_20, edge_weight, L0_gnn_W_in, L0_gnn_b_in, L0_gnn_W_f, L0_gnn_b_f, L0_gnn_W_out,
            L0_gnn_b_out):
    import numpy as np
    nodes, E = x.shape[0], src.shape[0]
    groups = -(-E // GE)
    pad = groups * GE - E
    nodes_pad = -(-(nodes + P) // (HS * QE)) * (HS * QE)
    src = np.pad(np.asarray(src), (0, pad), mode="edge")
    dst = np.pad(np.asarray(dst), (0, pad), mode="edge")
    w = np.pad(np.asarray(edge_weight), (0, pad))
    attr = np.pad(np.asarray(edge_attr_20), ((0, pad), (0, 0)))
    c = np.ascontiguousarray
    return {
        "xT": c(np.pad(np.asarray(x), ((0, nodes_pad - nodes), (0, 0))).T),
        "x": c(x),
        "dst_g": c(dst.reshape(groups, GE)),
        "src_nat": c(src.reshape(P, -1)),
        "src_col": c(src.reshape(-1, P).T),
        "dst_col": c(dst.reshape(-1, P).T),
        "w_col": c(w.reshape(-1, P).T),
        "attrT": c(attr.reshape(groups * GROUP, QUAD, P, -1).transpose(1, 3, 0, 2).reshape(-1, groups * GROUP * P)),
        "w_inT": c(np.asarray(L0_gnn_W_in).T),
        "b_in": c(np.tile(np.asarray(L0_gnn_b_in)[None, :], (P, 1))),
        "w_fT": c(np.asarray(L0_gnn_W_f).T),
        "b_f": c(np.asarray(L0_gnn_b_f)[None, :]),
        "w_outT": c(np.asarray(L0_gnn_W_out).T),
        "b_out": c(np.asarray(L0_gnn_b_out)[None, :]),
    }


def kernel(**inputs):
    import concourse.bacc as _bacc
    from concourse.bass_utils import run_bass_kernel_spmd as _run

    nc = _bacc.Bacc("TRN2", target_bir_lowering=False, num_devices=1)
    arrays = {f"in_{n}": a for n, a in layouts(**inputs).items()}
    args = [nc.dram_tensor(n, a.shape, mybir.dt.from_np(a.dtype), kind="ExternalInput").ap() for n, a in arrays.items()]
    out = nc.dram_tensor("out", inputs["x"].shape, F32, kind="ExternalOutput").ap()
    schnet_block(nc, *args, out)
    return _run(nc, [arrays], core_ids=[0]).results[0]["out"]
```

```python
from contextlib import ExitStack

import concourse.bass as bass
from concourse import mybir

ALU = mybir.AluOpType
ACT = mybir.ActivationFunctionType
AX_X = mybir.AxisListType.X
F32 = mybir.dt.float32
BF16 = mybir.dt.bfloat16
I32 = mybir.dt.int32

P = 128
QUAD = 4
QE = QUAD * P
GROUP = 2
GT = GROUP * QUAD
GE = GROUP * QE
REPLICAS = QUAD
CHUNKS = 8
IN_FLIGHT = 2
EPS = 1e-5
C_SRC, C_WEIGHT, C_DUMMY, C_NODE = 0, GT, 2 * GT, 3 * GT
COLS = 3 * GT + 1
CREDIT = 4
HS = 5


def after(k):
    return k + CREDIT + 1


def quad_of(i, j):
    return i * (2 * GROUP) + j


def group_of(i, j):
    return i * 2 + j // GROUP


def replica_flat(t, r):
    return t["dram"]["agg"][r].rearrange("(p a) f -> p (a f)", p=P).rearrange("p (b c) -> p b c", b=CHUNKS)


def clear_pieces(queue, t, r, pieces):
    for b in pieces:
        n = (r - 1) * CHUNKS + b
        signal = t["cleared"][n % IN_FLIGHT]
        if n >= IN_FLIGHT:
            queue.wait_ge(signal, n // IN_FLIGHT * 16)
        queue.dma_start(replica_flat(t, r)[:, b, :], t["sbuf"]["zeros"][:]).then_inc(signal, 16)


def wait_cleared(eng, t, r):
    if r == 0:
        eng.wait_ge(t["first_cleared"], 16)
    else:
        for place, signal in enumerate(t["cleared"]):
            eng.wait_ge(signal, -(-(r * CHUNKS - place) // IN_FLIGHT) * 16)


def prepare(nc, t):
    A_, S = t["dram"], t["sbuf"]
    cols_all, ident, tri = S["cols_all"], S["ident"], S["tri"]
    nodes_pad, tiles, groups = t["nodes_pad"], t["tiles"], t["groups"]
    blocks = -(-groups // P)
    hi_mask = (-(-t["nodes"] // P) * P - 1)
    hi_mask = (1 << hi_mask.bit_length()) - P
    nq = nodes_pad // QE
    passes = nq // HS
    NA = A_["w_fT"].shape[0]
    assert nq % HS == 0 and hi_mask < (1 << 15)

    with ExitStack() as ctx:
        def sb(name, shape, dt):
            return ctx.enter_context(nc.sbuf_tensor(f"{name}_sb", shape, dt))

        def sem(name):
            return ctx.enter_context(nc.semaphore(f"{name}_sem"))

        src_nat = sb("src_nat", [P, tiles], I32)
        src_hi_int = sb("src_hi_int", [P, tiles], I32)
        src_hi = sb("src_hi", [P, tiles], BF16)
        src_lo = sb("src_lo", [P, tiles], BF16)
        dst_hi_int = sb("dst_hi_int", [P, GE], I32)
        dst_hi = sb("dst_hi", [P, blocks, GE], BF16)
        dst_lo = sb("dst_lo", [P, blocks, GE], BF16)
        src_col = sb("src_col", [P, tiles], I32)
        w_col = sb("w_col", [P, tiles], F32)
        dst_g = sb("dst_g", [P, blocks, GE], I32)
        least = sb("least", [P, blocks], F32)
        most = sb("most", [P, blocks], F32)
        span = sb("span", [P, blocks], F32)
        wide = sb("wide", [P, blocks], F32)
        wide_any = sb("wide_any", [P, 1], F32)
        base_int = sb("base_int", [P, blocks], I32)
        base_bc = sb("base_bc", [P, groups], I32)
        part_i = sb("part_i", [P, 1], I32)
        part = sb("part", [P, 1], F32)
        dummy = sb("dummy_row", [P, 1], F32)
        ones_col = sb("ones_col", [P, 1], F32)
        ones_sq = sb("ones_sq", [P, P], F32)
        zeros = S["zeros"]
        xT = sb("xT", [P, HS, QE], F32)
        h_sb = sb("h_sb", [P, HS, QE], F32)
        w_in = sb("w_in", [P, P], F32)
        b_in = sb("b_in", [P, P], F32)
        h_ps = ctx.enter_context(nc.psum_tensor("h_ps", [P, HS, QE], F32))
        flag_ps = ctx.enter_context(nc.psum_tensor("flag_ps", [P, QE], F32))

        dstg_in, nat_in = sem("dstg_in"), sem("nat_in")
        col_in, w_in_sem, wts_in, tab_in = sem("col_in"), sem("w_in_sem"), sem("wts_in"), sem("tab_in")
        xT_in = [sem(f"xT_in{s}") for s in range(HS)]
        h_out = [sem(f"h_out{s}") for s in range(HS)]
        rows_out, base_out, base_in, basebc_in = (sem("rows_out"), sem("base_out"), sem("base_in"),
                                                  sem("basebc_in"))
        zeros_set, part_set, dummy_set = sem("zeros_set"), sem("part_set"), sem("dummy_set")
        lims_set, lims_done, span_done = (sem("lims_set"), sem("lims_done"),
                                                      sem("span_done"))
        base_done, flag_mm, flag_done, hi_masked = sem("base_done"), sem("flag_mm"), sem("flag_done"), sem("hi_masked")
        hi_done, lo_done, cols_set, h_mm, h_done = (sem("hi_done"), sem("lo_done"), sem("cols_set"), sem("h_mm"),
                                                    sem("h_done"))
        iota_done, sel_zero, sel_set = (sem("iota_done"), sem("sel_zero"),
                                                   sem("sel_set"))
        wf_zero, wf_in = sem("wf_zero"), sem("wf_in")
        masks_base, masks_done, weights_set = sem("masks_base"), sem("masks_done"), sem("weights_set")

        block = ctx.enter_context(nc.Block())

        @block.sync
        def _(sp):
            for b in range(blocks):
                n = min(P, groups - b * P)
                sp.dma_start(dst_g[0:n, b, :], A_["dst_g"][b * P:b * P + n]).then_inc(dstg_in, 16)
            sp.dma_start(src_nat[:], A_["src_nat"]).then_inc(nat_in, 16)
            sp.dma_start(w_in[:], A_["w_inT"]).then_inc(wts_in, 16)
            sp.dma_start(b_in[:], A_["b_in"]).then_inc(wts_in, 16)
            def load_x(i, s, again):
                if again:
                    sp.wait_ge(h_mm, i * HS + (s + 1 - HS))
                sp.dma_start(xT[:, s, :], A_["xT"][:, bass.ds(i * (HS * QE) + s * QE, QE)]).then_inc(xT_in[s], 16)

            for s in range(HS):
                load_x(0, s, False)
            sp.dma_start(src_col[:], A_["src_col"]).then_inc(col_in, 16)
            sp.dma_start(w_col[:], A_["w_col"]).then_inc(w_in_sem, 16)
            sp.wait_ge(base_done, 1)
            for b in range(blocks):
                n = min(P, groups - b * P)
                sp.dma_start(A_["bases"][b * P:b * P + n], base_int[0:n, b:b + 1]).then_inc(base_out, 16)
            with sp.Fori(1, passes) as i:
                for s in range(HS):
                    load_x(i, s, True)
            sp.wait_ge(base_out, 16 * blocks)
            bases_row = A_["bases"].rearrange("g a -> a g")
            sp.dma_start(S["base_row"][:], bases_row[:, 0:groups]).then_inc(base_in, 16)
            sp.dma_start(base_bc[:], bases_row[:, 0:groups].broadcast_to([P, groups])).then_inc(basebc_in, 16)
            sp.wait_ge(wf_zero, 1)
            for q in range(QUAD):
                sl = slice(q * P, (q + 1) * P)
                sp.dma_start(S["w_f"][q * NA:(q + 1) * NA, sl], A_["w_fT"]).then_inc(wf_in, 16)
                sp.dma_start(S["w_f"][QUAD * NA:QUAD * NA + 1, sl], A_["b_f"]).then_inc(wf_in, 16)
            sp.dma_start(S["w_out"][:], A_["w_outT"]).then_inc(tab_in, 16)
            sp.dma_start(S["b_out"][:], A_["b_out"]).then_inc(tab_in, 16)
            sp.wait_ge(zeros_set, 1)
            clear_pieces(sp, t, 1, range(IN_FLIGHT))
            sp.wait_ge(base_in, 16)
            sp.wait_ge(tab_in, 32)
            sp.wait_ge(wf_in, 32 * QUAD)

        @block.gpsimd
        def _(pool):
            nc.gpsimd.memset(zeros[:], 0.0).then_inc(zeros_set, 1)
            nc.gpsimd.iota(part_i[:], pattern=[[0, 1]], base=0, channel_multiplier=1).then_inc(iota_done, 1)
            nc.gpsimd.memset(ones_sq[:], 1.0).then_inc(masks_base, 1)
            pool.wait_ge(zeros_set, 1)
            again = zeros[:].rearrange("p (a f) -> p a f", a=1).broadcast_to([P, CHUNKS, nodes_pad // CHUNKS])
            pool.dma_start(replica_flat(t, 0), again).then_inc(t["first_cleared"], 16)
            pool.wait_ge(masks_base, 1)
            nc.gpsimd.affine_select(out=tri[:], in_=ones_sq[:], compare_op=ALU.is_ge, fill=0.0, base=0,
                                    pattern=[[-1, P]], channel_multiplier=1).then_inc(masks_done, 1)
            nc.gpsimd.affine_select(out=ident[:], in_=ones_sq[:], compare_op=ALU.is_equal, fill=0.0, base=0,
                                    pattern=[[-1, P]], channel_multiplier=1).then_inc(masks_done, 1)
            pool.wait_ge(w_in_sem, 16)
            nc.gpsimd.tensor_copy(cols_all[:, :, C_WEIGHT:C_WEIGHT + GT],
                                  w_col[:].rearrange("p (g t) -> p g t", t=GT)).then_inc(weights_set, 1)
            pool.wait_ge(weights_set, 1)
            pool.wait_ge(masks_done, 2)

        @block.scalar
        def _(act):
            def store_rows(r, half):
                act.dma_start(A_["rows"][r].rearrange("(p c) -> p c", p=P), half[:]).then_inc(rows_out, 16)

            def store_blocks(r, half):
                by_group = A_["rows"][r].rearrange("(g e) -> g e", e=GE)
                for b in range(blocks):
                    n = min(P, groups - b * P)
                    act.dma_start(by_group[b * P:b * P + n], half[0:n, b, :]).then_inc(rows_out, 16)

            for b in range(blocks):
                n = min(P, groups - b * P)
                act.wait_ge(hi_masked, b + 1)
                nc.scalar.copy(dst_hi[0:n, b, :], dst_hi_int[0:n, :]).then_inc(hi_done, 1)
            act.wait_ge(hi_masked, blocks + 1)
            nc.scalar.copy(src_hi[:], src_hi_int[:]).then_inc(hi_done, 1)
            act.wait_ge(hi_done, blocks + 1)
            act.wait_ge(lo_done, blocks + 1)
            store_rows(0, src_hi)
            store_rows(1, src_lo)
            store_blocks(2, dst_hi)
            store_blocks(3, dst_lo)

            def store_h(i, s):
                act.wait_ge(h_done, i * HS + (s + 1))
                rows = A_["h"][bass.ds(i * (HS * QE) + s * QE, QE)].rearrange("(p t) f -> p (t f)", t=QUAD)
                act.dma_start(rows, h_sb[:, s, :]).then_inc(h_out[s], 16)

            with act.Fori(0, passes) as i:
                for s in range(HS):
                    store_h(i, s)
            for s in range(HS):
                act.wait_ge(h_out[s], 16 * passes)
            act.wait_ge(rows_out, 32 * (blocks + 1))

        @block.tensor
        def _(pe):
            pe.wait_ge(wts_in, 32)

            def products(i, s, again):
                pe.wait_ge(xT_in[s], i * 16 + 16)
                if again:
                    pe.wait_ge(h_done, i * HS + (s + 1 - HS))
                x_s = xT[:, s, :].rearrange("k (p t) -> k p t", t=QUAD)
                for q in range(QUAD):
                    mm = nc.tensor.matmul(h_ps[:, s, q * P:(q + 1) * P], x_s[:, :, q], w_in[:], start=True, stop=True)
                mm.then_inc(h_mm, 1)

            for s in range(HS):
                products(0, s, False)
            with pe.Fori(1, passes) as i:
                for s in range(HS):
                    products(i, s, True)
            pe.wait_ge(span_done, 3)
            nc.tensor.matmul(flag_ps[0:1, 0:1], wide_any[:], ones_col[:], start=True, stop=True).then_inc(flag_mm, 1)

        @block.vector
        def _(dve):
            nc.vector.memset(S["w_f"][:], 0.0).then_inc(wf_zero, 1)
            nc.vector.memset(least[:], 0.0).then_inc(lims_set, 1)
            nc.vector.memset(most[:], 0.0).then_inc(lims_set, 1)
            nc.vector.memset(ones_col[:], 1.0)
            nc.vector.memset(S["ones_row"][:], 1.0)
            nc.vector.memset(S["half"][:], 0.5)
            nc.vector.memset(S["minus_half"][:], -0.5)
            nc.vector.memset(S["attr"][:], 1.0)
            nc.vector.memset(S["sel_src"][:], 0.0).then_inc(sel_zero, 1)
            nc.vector.memset(S["sel_dst"][:], 1.0).then_inc(sel_zero, 1)
            dve.wait_ge(sel_zero, 2)
            nc.vector.memset(S["sel_src"][0:2, :], 1.0)
            nc.vector.memset(S["sel_dst"][0:2, :], 0.0).then_inc(sel_set, 1)
            dve.wait_ge(dstg_in, 16 * blocks)
            dve.wait_ge(lims_set, 2)
            for b in range(blocks):
                n = min(P, groups - b * P)
                nc.vector.tensor_reduce(least[0:n, b:b + 1], dst_g[0:n, b, :], AX_X, ALU.min).then_inc(lims_done, 1)
                nc.vector.tensor_reduce(most[0:n, b:b + 1], dst_g[0:n, b, :], AX_X, ALU.max).then_inc(lims_done, 1)
            dve.wait_ge(lims_done, 2 * blocks)
            nc.vector.tensor_copy(base_int[:], least[:]).then_inc(base_done, 1)
            nc.vector.tensor_tensor(span[:], most[:], least[:], ALU.subtract).then_inc(span_done, 1)
            dve.wait_ge(span_done, 1)
            nc.vector.tensor_scalar(wide[:], span[:], float(P - 1), None, ALU.is_gt).then_inc(span_done, 1)
            dve.wait_ge(span_done, 2)
            nc.vector.tensor_reduce(wide_any[:], wide[:], AX_X, ALU.add).then_inc(span_done, 1)

            for b in range(blocks):
                n = min(P, groups - b * P)
                if b:
                    dve.wait_ge(hi_done, b)
                    dve.wait_ge(lo_done, b)
                nc.vector.tensor_scalar(dst_hi_int[0:n, :], dst_g[0:n, b, :], hi_mask, None,
                                        ALU.bitwise_and).then_inc(hi_masked, 1)
                dve.wait_ge(hi_masked, b + 1)
                nc.vector.tensor_tensor(dst_lo[0:n, b, :], dst_g[0:n, b, :], dst_hi_int[0:n, :],
                                        ALU.subtract).then_inc(lo_done, 1)
            dve.wait_ge(nat_in, 16)
            nc.vector.tensor_scalar(src_hi_int[:], src_nat[:], hi_mask, None, ALU.bitwise_and).then_inc(hi_masked, 1)
            dve.wait_ge(hi_masked, blocks + 1)
            nc.vector.tensor_tensor(src_lo[:], src_nat[:], src_hi_int[:], ALU.subtract).then_inc(lo_done, 1)

            dve.wait_ge(iota_done, 1)
            nc.vector.tensor_copy(part[:], part_i[:]).then_inc(part_set, 1)
            dve.wait_ge(part_set, 1)
            nc.vector.tensor_scalar(dummy[:], part[:], float(t["nodes"]), None, ALU.add).then_inc(dummy_set, 1)

            def add_bias(i, s, again):
                dve.wait_ge(h_mm, i * HS + (s + 1))
                if again:
                    dve.wait_ge(h_out[s], i * 16)
                nc.vector.tensor_tensor(h_sb[:, s, :].rearrange("p (t f) -> p t f", t=QUAD),
                                        h_ps[:, s, :].rearrange("p (t f) -> p t f", t=QUAD),
                                        b_in[:].rearrange("p (a f) -> p a f", a=1).broadcast_to([P, QUAD, P]),
                                        ALU.add).then_inc(h_done, 1)

            dve.wait_ge(wts_in, 32)
            for s in range(HS):
                add_bias(0, s, False)
            with dve.Fori(1, passes) as i:
                for s in range(HS):
                    add_bias(i, s, True)

            dve.wait_ge(col_in, 16)
            nc.vector.tensor_copy(cols_all[:, :, C_SRC:C_SRC + GT],
                                  src_col[:].rearrange("p (g t) -> p g t", t=GT)).then_inc(cols_set, 1)
            dve.wait_ge(dummy_set, 1)
            nc.vector.tensor_scalar(cols_all[:, :, C_DUMMY:C_DUMMY + GT],
                                    src_col[:].rearrange("p (g t) -> p g t", t=GT), -1.0, dummy[:, 0:1],
                                    ALU.mult, ALU.add).then_inc(cols_set, 1)
            dve.wait_ge(flag_mm, 1)
            nc.vector.tensor_copy(S["flag"][:], flag_ps[0:1, 0:1]).then_inc(flag_done, 1)
            dve.wait_ge(basebc_in, 16)
            nc.vector.tensor_scalar(cols_all[:, :, C_NODE], base_bc[:], part[:, 0:1], None,
                                    ALU.add).then_inc(cols_set, 1)
            dve.wait_ge(cols_set, 3)
            dve.wait_ge(flag_done, 1)
            dve.wait_ge(sel_set, 1)


def edges(nc, t):
    A_, S = t["dram"], t["sbuf"]
    cols_all, dst_all, ident, tri = S["cols_all"], S["dst_all"], S["ident"], S["tri"]
    groups = t["groups"]
    quads = groups * GROUP
    passes = (groups - 1) // 2
    rest = quads - 4 * passes
    assert passes > t["nq"]

    with ExitStack() as ctx:
        def sb(name, shape, dt):
            return ctx.enter_context(nc.sbuf_tensor(f"{name}_sb", shape, dt))

        def psum(name, shape):
            return ctx.enter_context(nc.psum_tensor(name, shape, F32))

        def sem(name):
            return ctx.enter_context(nc.semaphore(f"{name}_sem"))

        attr = S["attr"]
        KA = attr.shape[0]
        rows = sb("rows", [4, 2, GE], BF16)
        window = sb("window", [P, 2, P], F32)
        cols = sb("cols", [P, 2, COLS], F32)
        dst_i = sb("dst_i", [P, 2, GT], I32)
        onehot = sb("onehot", [P, 2, QE], F32)
        merge = sb("merge", [P, 4, QE], F32)
        count = sb("count", [P, 2, QUAD], F32)
        moved = sb("moved", [P, 2, QUAD], F32)
        target = sb("target", [P, 4, QUAD], I32)
        size = sb("size", [P, 2, QE], F32)
        expo = sb("expo", [P, 2, QE], F32)
        logp = sb("logp", [P, 2, QE], F32)
        filt = sb("filt", [P, QE], F32)
        gath = sb("gath", [P, 2, QE], F32)
        msg = sb("msg", [P, 2, QE], F32)
        stage = sb("stage", [P, 4, QE], F32)
        src_ps = psum("src_ps", [P, QE])
        dst_ps = psum("dst_ps", [P, QE])
        filt_ps = psum("filt_ps", [P, 2, QE])
        gath_ps = psum("gath_ps", [P, 2, QE])
        sum_ps = psum("sum_ps", [P, 2, QE])

        dst_all_in = sem("dst_all_in")
        loads_in = [sem(f"loads_in{s}") for s in range(2)]
        gathered = [sem(f"gathered{s}") for s in range(2)]
        scattered = [sem(f"scattered{r}") for r in range(REPLICAS)]
        spread_done = sem("spread_done")
        onehot_done = sem("onehot_done")
        merge_done = sem("merge_done")
        target_done = sem("target_done")
        gather_done = sem("gather_done")
        linear_done = sem("linear_done")
        size_done, exp_done, log_done = sem("size_done"), sem("exp_done"), sem("log_done")
        filt_done = sem("filt_done")
        msg_done = sem("msg_done")
        sum_done = sem("sum_done")
        stage_done = sem("stage_done")
        landed = sem("landed")
        rows_asked = sem("rows_asked")
        moved_done = sem("moved_done")
        cols_done = sem("cols_done")
        tail_zero = sem("tail_zero")

        block = ctx.enter_context(nc.Block())

        def both_ways(eng, body):
            wide = eng.value_load(S["flag"][0:1, 0:1], min_val=0, max_val=groups)
            with eng.If(wide == 0):
                body(True)
            with eng.Else():
                body(False)

        def steps(eng, step, local, head=()):
            for j in head:
                step(0, j, local)
            with eng.Fori(0, passes) as i:
                for j in range(4):
                    step(i, j, local)
            for j in range(rest):
                step(passes, j, local, last=True)

        def beyond(j, last):
            return last and j >= rest

        @block.sync
        def _(sp):
            def load(i, g, local):
                s = g % 2
                group = i * 2 + g
                sp.wait_ge(linear_done, after((group - 2) * GROUP + 1))
                sp.wait_ge(spread_done, after((group - 2) * GROUP + 1))
                sp.dma_start(attr[0:KA - 1, s, :], A_["attrT"][:, bass.ds(group * (GROUP * P), GROUP * P)]
                             ).then_inc(loads_in[s], 16)
                sp.dma_start(rows[:, s, :], A_["rows"][:, bass.ds(group * GE, GE)]).then_inc(loads_in[s], 16)
                if local:
                    sp.wait_ge(gather_done, after((group - 2) * GROUP + 1))
                    base = sp.value_load(S["base_row"][0:1, bass.ds(group, 1)], min_val=0, max_val=t["nodes"] - 1)
                    sp.dma_start(window[:, s, :], A_["h"][bass.ds(base, P)]).then_inc(loads_in[s], 16)

            def body(local):
                if not local:
                    sp.dma_start(dst_all[:], A_["dst_col"]).then_inc(dst_all_in, 16)
                for g in range(2):
                    load(0, g, local)
                clear_pieces(sp, t, 1, range(IN_FLIGHT, CHUNKS))
                load(1, 0, local)
                clear_pieces(sp, t, 2, range(CHUNKS))
                load(1, 1, local)
                clear_pieces(sp, t, 3, range(CHUNKS))
                with sp.Fori(2, passes) as i:
                    for g in range(2):
                        load(i, g, local)
                for g in range(rest // GROUP):
                    load(passes, g, local)

            both_ways(sp, body)

        def loads(local):
            return 48 if local else 32

        @block.tensor
        def _(pe):
            for s in (spread_done, gather_done, linear_done, sum_done):
                pe.sem_inc(s, CREDIT)

            def arrived(i, j, local):
                pe.wait_ge(loads_in[(j // GROUP) % 2], (i + (j // GROUP) // 2 + 1) * loads(local))

            def spread(i, j, local):
                k, g, e = quad_of(i, j), (j // GROUP) % 2, (j % GROUP) * QE
                arrived(i, j, local)
                pe.wait_ge(merge_done, after(k - 1))
                nc.tensor.matmul(src_ps[:], S["sel_src"][:], rows[:, g, e:e + QE], start=True, stop=True)
                if local:
                    pe.wait_ge(onehot_done, after(k - 1))
                mm = nc.tensor.matmul(dst_ps[:], S["sel_dst"][:], rows[:, g, e:e + QE], start=True, stop=True)
                mm.then_inc(spread_done, 1)

            def linear(i, j, local):
                k, g, e = quad_of(i, j), (j // GROUP) % 2, (j % GROUP) * P
                arrived(i, j, local)
                pe.wait_ge(filt_done, after(k - 2))
                mm = nc.tensor.matmul(filt_ps[:, j % 2, :], attr[:, g, e:e + P], S["w_f"][:], start=True, stop=True)
                mm.then_inc(linear_done, 1)

            def gather(i, j, local):
                k, g = quad_of(i, j), (j // GROUP) % 2
                pe.wait_ge(onehot_done, after(k))
                pe.wait_ge(msg_done, after(k - 2))
                for q in range(QUAD):
                    mm = nc.tensor.matmul(gath_ps[:, j % 2, q * P:(q + 1) * P], onehot[:, j % 2, q * P:(q + 1) * P],
                                          window[:, g, :], start=True, stop=True)
                mm.then_inc(gather_done, 1)

            def merge_sources(i, j):
                k = quad_of(i, j)
                pe.wait_ge(merge_done, after(k))
                pe.wait_ge(msg_done, after(k))
                pe.wait_ge(stage_done, after(k - 2))
                for q in range(QUAD):
                    sl = slice(q * P, (q + 1) * P)
                    mm = nc.tensor.matmul(sum_ps[:, j % 2, sl], merge[:, j % 4, sl], msg[:, j % 2, sl],
                                          start=True, stop=True)
                mm.then_inc(sum_done, 1)

            def step(i, j, local, last=False):
                if local and not beyond(j + 1, last):
                    gather(i, j + 1, local)
                if not beyond(j + 2, last):
                    spread(i, j + 2, local)
                    linear(i, j + 2, local)
                if j >= 0:
                    merge_sources(i, j)

            def body(local):
                spread(0, 0, local)
                linear(0, 0, local)
                steps(pe, step, local, head=(-1,))

            both_ways(pe, body)

        @block.vector
        def _(dve):
            for s in (onehot_done, merge_done, target_done, filt_done, msg_done, moved_done, cols_done):
                dve.sem_inc(s, CREDIT)

            def begin(i, j, local):
                k, s, g, c = quad_of(i, j), j % 2, (j // GROUP) % 2, (j % GROUP) * QUAD
                group = group_of(i, j)
                if j % GROUP == 0:
                    dve.wait_ge(msg_done, after(k - 3))
                    if not local:
                        nc.vector.tensor_copy(dst_i[:, g, :], dst_all[:, bass.ds(group * GT, GT)])
                    nc.vector.tensor_copy(cols[:, g, :], cols_all[:, bass.ds(group, 1), :].rearrange("p a c -> p (a c)")
                                          ).then_inc(cols_done, 1)
                dve.wait_ge(cols_done, after(group))
                dve.wait_ge(spread_done, after(k))
                if local:
                    dve.wait_ge(gather_done, after(k - 2))
                    nc.vector.tensor_scalar(onehot[:, s, :], dst_ps[:], cols[:, g, C_NODE:C_NODE + 1], None,
                                            ALU.is_equal).then_inc(onehot_done, 1)
                dve.wait_ge(sum_done, after(k - 4))
                for q in range(QUAD):
                    sl = slice(q * P, (q + 1) * P)
                    ins = nc.vector.scalar_tensor_tensor(out=merge[:, j % 4, sl], in0=src_ps[:, sl],
                                                         scalar=cols[:, g, C_SRC + c + q:C_SRC + c + q + 1],
                                                         in1=tri[:], op0=ALU.is_equal, op1=ALU.mult,
                                                         accum_out=count[:, s, q:q + 1])
                ins.then_inc(merge_done, 1)

            def targets_a(i, j):
                k, s, g, c = quad_of(i, j), j % 2, (j // GROUP) % 2, (j % GROUP) * QUAD
                dve.wait_ge(merge_done, after(k))
                nc.vector.scalar_tensor_tensor(out=moved[:, s, :], in0=count[:, s, :], scalar=1.5,
                                               in1=cols[:, g, C_DUMMY + c:C_DUMMY + c + QUAD],
                                               op0=ALU.is_gt, op1=ALU.mult).then_inc(moved_done, 1)

            def targets_b(i, j):
                k, s, g, c = quad_of(i, j), j % 2, (j // GROUP) % 2, (j % GROUP) * QUAD
                dve.wait_ge(moved_done, after(k))
                dve.wait_ge(landed, after(k - 4) * QUAD)
                nc.vector.tensor_tensor(target[:, j % 4, :], moved[:, s, :], cols[:, g, C_SRC + c:C_SRC + c + QUAD],
                                        ALU.add).then_inc(target_done, 1)

            def softplus(i, j):
                k, s = quad_of(i, j), j % 2
                dve.wait_ge(log_done, after(k))
                dve.wait_ge(msg_done, after(k - 1))
                nc.vector.scalar_tensor_tensor(out=filt[:], in0=filt_ps[:, s, :], scalar=0.0, in1=logp[:, s, :],
                                               op0=ALU.max, op1=ALU.add).then_inc(filt_done, 1)

            def messages(i, j, local):
                k, s, g, c = quad_of(i, j), j % 2, (j // GROUP) % 2, (j % GROUP) * QUAD
                dve.wait_ge(filt_done, after(k))
                if local:
                    dve.wait_ge(gather_done, after(k))
                else:
                    dve.wait_ge(gathered[s], (i * 2 + j // 2 + 1) * (16 * QUAD))
                dve.wait_ge(sum_done, after(k - 2))
                rows_of_h = gath_ps if local else gath
                for q in range(QUAD):
                    sl = slice(q * P, (q + 1) * P)
                    ins = nc.vector.scalar_tensor_tensor(out=msg[:, s, sl], in0=filt[:, sl],
                                                         scalar=cols[:, g, C_WEIGHT + c + q:C_WEIGHT + c + q + 1],
                                                         in1=rows_of_h[:, s, sl], op0=ALU.mult, op1=ALU.mult)
                ins.then_inc(msg_done, 1)

            def step(i, j, local, last=False):
                more = not beyond(j + 1, last)
                if more:
                    begin(i, j + 1, local)
                if j >= 0:
                    softplus(i, j)
                if more:
                    targets_a(i, j + 1)
                if j >= 0:
                    messages(i, j, local)
                if more:
                    targets_b(i, j + 1)

            def body(local):
                if not local:
                    dve.wait_ge(dst_all_in, 16)
                steps(dve, step, local, head=(-1,))

            both_ways(dve, body)

        @block.scalar
        def _(act):
            for s in (size_done, exp_done, log_done, stage_done):
                act.sem_inc(s, CREDIT)

            def chain(i, j):
                k, s = quad_of(i, j), j % 2
                act.wait_ge(linear_done, after(k))
                act.wait_ge(exp_done, after(k - 2))
                nc.scalar.activation(size[:, s, :], filt_ps[:, s, :], ACT.Abs).then_inc(size_done, 1)
                act.wait_ge(size_done, after(k))
                act.wait_ge(log_done, after(k - 2))
                nc.scalar.activation(expo[:, s, :], size[:, s, :], ACT.Exp, scale=-1.0).then_inc(exp_done, 1)
                act.wait_ge(exp_done, after(k))
                act.wait_ge(filt_done, after(k - 2))
                nc.scalar.activation(logp[:, s, :], expo[:, s, :], ACT.Ln, bias=S["half"][:, 0:1],
                                     scale=0.5).then_inc(log_done, 1)

            def stage_sums(i, j):
                k = quad_of(i, j)
                act.wait_ge(sum_done, after(k))
                act.wait_ge(landed, after(k - 4) * QUAD)
                nc.scalar.copy(stage[:, j % 4, :], sum_ps[:, j % 2, :]).then_inc(stage_done, 1)

            def step(i, j, local, last=False):
                if not beyond(j + 1, last):
                    chain(i, j + 1)
                if j >= 0:
                    stage_sums(i, j)

            nc.scalar.preload_act_table_set("natural_log_exp_and_others")
            def load_x(q, n):
                act.dma_start(S["x_all"][0:n, bass.ds(q, 1), :].rearrange("p a f -> p (a f)"),
                              A_["x"][bass.ds(q * QE, n * QUAD)].rearrange("(p t) f -> p (t f)", t=QUAD)
                              ).then_inc(t["x_in"], 16)

            def body(local):
                full = t["nq"] - 1
                for j in range(-1, 4):
                    step(0, j, local)
                act.wait_ge(tail_zero, 1)
                load_x(full, t["tail"] // QUAD)
                with act.Fori(1, 1 + full) as i:
                    load_x(i - 1, P)
                    for j in range(4):
                        step(i, j, local)
                with act.Fori(1 + full, passes) as i:
                    for j in range(4):
                        step(i, j, local)
                for j in range(rest):
                    step(passes, j, local, last=True)

            both_ways(act, body)

        @block.gpsimd
        def _(pool):
            nc.gpsimd.memset(S["x_all"][:, t["nq"] - 1, :], 0.0).then_inc(tail_zero, 1)
            pool.sem_inc(landed, CREDIT * QUAD)

            def gather_rows(i, j):
                k, s, g, c = quad_of(i, j), j % 2, (j // GROUP) % 2, (j % GROUP) * QUAD
                pool.wait_ge(cols_done, after(group_of(i, j)))
                pool.wait_ge(msg_done, after(k - 2))
                pool.sem_inc(rows_asked, 1)
                for q in range(QUAD):
                    nc.gpsimd.indirect_dma_start(
                        gath[:, s, q * P:(q + 1) * P], None, A_["h"],
                        bass.IndirectOffsetOnAxis(ap=dst_i[:, g, c + q:c + q + 1], axis=0)).then_inc(gathered[s], 16)

            def add_tile(j, q, r):
                nc.gpsimd.indirect_dma_start(
                    A_["agg"][r], bass.IndirectOffsetOnAxis(ap=target[:, j % 4, q:q + 1], axis=0),
                    stage[:, j % 4, q * P:(q + 1) * P], None, compute_op=ALU.add).then_inc(scattered[r], 16)

            def add_head(j):
                pool.wait_ge(target_done, after(j))
                pool.wait_ge(stage_done, after(j))
                for q in range(QUAD):
                    r, before = q % 2, (j * QUAD + q) // 2
                    if before:
                        pool.wait_ge(scattered[r], before * 16)
                    else:
                        wait_cleared(pool, t, r)
                    if j:
                        pool.sem_inc(landed, 1)
                    add_tile(j, q, r)

            def adds_before(k, r):
                return k + 4 if r < 2 else k - 4

            def add(i, j, new):
                k = quad_of(i, j)
                pool.wait_ge(target_done, after(k))
                pool.wait_ge(stage_done, after(k))
                for q in range(QUAD):
                    if new and q >= 2:
                        wait_cleared(pool, t, q)
                    else:
                        pool.wait_ge(scattered[q], adds_before(k, q) * 16)
                    pool.sem_inc(landed, 1)
                    add_tile(j, q, q)

            def step(i, j, local, last=False, head=False, new=False):
                if not local and not beyond(j + 1, last):
                    gather_rows(i, j + 1)
                if head:
                    add_head(j)
                else:
                    add(i, j, new)

            def body(local):
                if not local:
                    gather_rows(0, 0)
                for j in range(4):
                    step(0, j, local, head=True)
                for j in range(4):
                    step(1, j, local, new=(j == 0))
                with pool.Fori(2, passes) as i:
                    for j in range(4):
                        step(i, j, local)
                for j in range(rest):
                    step(passes, j, local, last=True)
                for q in range(REPLICAS):
                    pool.wait_ge(scattered[q], adds_before(quads, q) * 16)

            both_ways(pool, body)


def finish(nc, t):
    A_, S = t["dram"], t["sbuf"]
    ident = S["ident"]
    nq, tail = t["nq"], t["tail"]
    passes = (nq - 4) // 4
    rest = nq - 4 * passes

    with ExitStack() as ctx:
        def sb(name, shape, dt=F32):
            return ctx.enter_context(nc.sbuf_tensor(f"{name}_sb", shape, dt))

        def psum(name, shape):
            return ctx.enter_context(nc.psum_tensor(name, shape, F32))

        def sem(name):
            return ctx.enter_context(nc.semaphore(f"{name}_sem"))

        part_sum = sb("part_sum", [P, 4, REPLICAS, QE])
        pair_a = sb("pair_a", [P, 2, QE])
        pair_b = sb("pair_b", [P, 2, QE])
        aggT = sb("aggT", [P, 2, QE])
        size = sb("n_size", [P, 2, QE])
        expo = sb("n_expo", [P, 2, QE])
        logp = sb("n_logp", [P, 2, QE])
        soft = sb("soft", [P, QE])
        res = sb("res", [P, 2, QE])
        stats = sb("stats", [P, QUAD, 6])
        moments = sb("moments", [P, 2, QUAD, 2])
        rstd = sb("rstd", [P, 2, QUAD])
        varep = sb("varep", [P, 2, QUAD])
        shift = sb("shift", [P, 2, QUAD])
        normed = sb("normed", [P, 4, QE])
        aggT_ps = psum("aggT_ps", [P, 2, QE])
        out_ps = psum("out_ps", [P, 2, QE])

        parts_in = [sem(f"parts_in{s}") for s in range(4)]
        stored = [sem(f"stored{s}") for s in range(4)]
        pair_done = sem("pair_done")
        turned, turned_sb, linear_done = sem("turned"), sem("turned_sb"), sem("n_linear_done")
        size_done, exp_done, log_done = sem("n_size_done"), sem("n_exp_done"), sem("n_log_done")
        soft_done, res_done, stats_done, moments_done = (sem("soft_done"), sem("res_done"), sem("stats_done"),
                                                         sem("moments_done"))
        shift_done, norm_b_done, stats_seen = sem("shift_done"), sem("norm_b_done"), sem("stats_seen")
        varep_done, rstd_done, norm_done = sem("varep_done"), sem("rstd_done"), sem("norm_done")
        block = ctx.enter_context(nc.Block())

        def steps(eng, step, head=()):
            for j in head:
                step(0, j)
            with eng.Fori(0, passes) as i:
                for j in range(4):
                    step(i, j)
            for j in range(rest):
                step(passes, j, last=True)

        def beyond(j, last):
            return last and j >= rest

        @block.sync
        def _(sp):
            def step(i, j, last=False):
                k, s = quad_of(i, j), j % 4
                sp.wait_ge(pair_done, after(k - 4))
                for r in range(REPLICAS):
                    sp.dma_start(part_sum[:, s, r, :], A_["agg"][r][bass.ds(k * QE, QE)].rearrange(
                        "(p t) f -> p (t f)", t=QUAD)).then_inc(parts_in[s], 16)

            steps(sp, step)

        @block.gpsimd
        def _(pool):
            for s in (pair_done, rstd_done):
                pool.sem_inc(s, CREDIT)

            def add_pair(i, j):
                k, s = quad_of(i, j), j % 4
                pool.wait_ge(parts_in[s], (i + j // 4 + 1) * (16 * REPLICAS))
                pool.wait_ge(turned, after(k - 2))
                nc.gpsimd.tensor_tensor(pair_a[:, j % 2, :], part_sum[:, s, 0, :], part_sum[:, s, 1, :], ALU.add)
                nc.gpsimd.tensor_tensor(pair_b[:, j % 2, :], part_sum[:, s, 2, :], part_sum[:, s, 3, :],
                                        ALU.add).then_inc(pair_done, 1)

            def step(i, j, last=False):
                if not beyond(j + 4, last):
                    add_pair(i, j + 4)
                k = quad_of(i, j)
                pool.wait_ge(varep_done, after(k))
                nc.gpsimd.tensor_tensor(rstd[:, j % 2, :], varep[:, j % 2, :], S["minus_half"][:],
                                        ALU.pow).then_inc(rstd_done, 1)

            for j in range(4):
                add_pair(0, j)
            steps(pool, step)

        @block.tensor
        def _(pe):
            for s in (turned, linear_done):
                pe.sem_inc(s, CREDIT)

            def turn(i, j):
                k, s = quad_of(i, j), j % 2
                pe.wait_ge(pair_done, after(k))
                pe.wait_ge(turned_sb, after(k - 2))
                for q in range(QUAD):
                    sl = slice(q * P, (q + 1) * P)
                    nc.tensor.matmul(aggT_ps[:, s, sl], pair_a[:, s, sl], ident[:], start=True, stop=False)
                    mm = nc.tensor.matmul(aggT_ps[:, s, sl], pair_b[:, s, sl], ident[:], start=False, stop=True)
                mm.then_inc(turned, 1)

            def linear(i, j):
                k, s = quad_of(i, j), j % 2
                pe.wait_ge(turned_sb, after(k))
                pe.wait_ge(soft_done, after(k - 2))
                for q in range(QUAD):
                    sl = slice(q * P, (q + 1) * P)
                    nc.tensor.matmul(out_ps[:, s, sl], aggT[:, s, sl], S["w_out"][:], start=True, stop=False)
                    mm = nc.tensor.matmul(out_ps[:, s, sl], S["ones_row"][:], S["b_out"][:], start=False, stop=True)
                mm.then_inc(linear_done, 1)

            def step(i, j, last=False):
                if not beyond(j + 3, last):
                    turn(i, j + 3)
                if j + 2 >= 0 and not beyond(j + 2, last):
                    linear(i, j + 2)

            steps(pe, step, head=(-3, -2, -1))

        @block.scalar
        def _(act):
            nc.scalar.preload_act_table_set("natural_log_exp_and_others")
            for s in (turned_sb, size_done, exp_done, log_done, norm_b_done):
                act.sem_inc(s, CREDIT)

            def copy_turned(i, j):
                k, s = quad_of(i, j), j % 2
                act.wait_ge(turned, after(k))
                act.wait_ge(linear_done, after(k - 2))
                nc.scalar.copy(aggT[:, s, :], aggT_ps[:, s, :]).then_inc(turned_sb, 1)

            def chain(i, j):
                k, s = quad_of(i, j), j % 2
                act.wait_ge(linear_done, after(k))
                act.wait_ge(exp_done, after(k - 2))
                nc.scalar.activation(size[:, s, :], out_ps[:, s, :], ACT.Abs).then_inc(size_done, 1)
                act.wait_ge(size_done, after(k))
                act.wait_ge(log_done, after(k - 2))
                nc.scalar.activation(expo[:, s, :], size[:, s, :], ACT.Exp, scale=-1.0).then_inc(exp_done, 1)
                act.wait_ge(exp_done, after(k))
                act.wait_ge(soft_done, after(k - 2))
                nc.scalar.activation(logp[:, s, :], expo[:, s, :], ACT.Ln, bias=S["half"][:, 0:1],
                                     scale=0.5).then_inc(log_done, 1)

            def normalise(i, j, again):
                k, s = quad_of(i, j), j % 2
                act.wait_ge(shift_done, after(k))
                if again:
                    act.wait_ge(stored[j % 4], (i + j // 4) * 16)
                for q in range(QUAD // 2, QUAD):
                    sl = slice(q * P, (q + 1) * P)
                    ins = nc.scalar.activation(normed[:, j % 4, sl], res[:, s, sl], ACT.Identity,
                                               bias=shift[:, s, q:q + 1], scale=rstd[:, s, q:q + 1])
                ins.then_inc(norm_b_done, 1)

            def store(i, j, last=False):
                k, s = quad_of(i, j), j % 4
                n = tail // QUAD if last and j == rest - 1 else P
                act.wait_ge(norm_done, after(k))
                act.wait_ge(norm_b_done, after(k))
                act.dma_start(A_["out"][bass.ds(k * QE, n * QUAD)].rearrange("(p t) f -> p (t f)", t=QUAD),
                              normed[0:n, s, :]).then_inc(stored[s], 16)

            def step(i, j, last=False, again=True):
                if not beyond(j + 3, last):
                    copy_turned(i, j + 3)
                if j + 2 >= 0 and not beyond(j + 2, last):
                    chain(i, j + 2)
                if j >= 0:
                    normalise(i, j, again)
                    store(i, j, last)

            for j in range(-3, 4):
                step(0, j, again=False)
            with act.Fori(1, passes) as i:
                for j in range(4):
                    step(i, j)
            for j in range(rest):
                step(passes, j, last=True)
            for s in range(4):
                act.wait_ge(stored[s], 16 * -(-(nq - s) // 4))

        @block.vector
        def _(dve):
            for s in (soft_done, res_done, stats_done, moments_done, varep_done, shift_done, norm_done):
                dve.sem_inc(s, CREDIT)

            def softplus(i, j):
                k, s = quad_of(i, j), j % 2
                dve.wait_ge(log_done, after(k))
                dve.wait_ge(res_done, after(k - 1))
                nc.vector.scalar_tensor_tensor(out=soft[:], in0=out_ps[:, s, :], scalar=0.0, in1=logp[:, s, :],
                                               op0=ALU.max, op1=ALU.add).then_inc(soft_done, 1)

            def residual(i, j):
                k, s = quad_of(i, j), j % 2
                dve.wait_ge(soft_done, after(k))
                dve.wait_ge(norm_b_done, after(k - 2))
                nc.vector.tensor_tensor(res[:, s, :], soft[:], S["x_all"][:, bass.ds(k, 1), :].rearrange(
                    "p a f -> p (a f)"), ALU.add).then_inc(res_done, 1)
                dve.wait_ge(res_done, after(k))
                for q in range(QUAD):
                    ins = nc.vector.bn_stats(stats[:, q, :], res[:, s, q * P:(q + 1) * P])
                ins.then_inc(stats_done, 1)
                dve.wait_ge(stats_done, after(k))
                dve.sem_inc(stats_seen, 1)
                for q in range(QUAD):
                    ins = nc.vector.bn_aggr(moments[:, s, q, :], stats[:, q, :])
                ins.then_inc(moments_done, 1)
                dve.wait_ge(moments_done, after(k))
                nc.vector.tensor_scalar(varep[:, s, :], moments[:, s, :, 1], EPS, None, ALU.add).then_inc(varep_done, 1)

            def normalise(i, j, again):
                k, s = quad_of(i, j), j % 2
                dve.wait_ge(rstd_done, after(k))
                nc.vector.scalar_tensor_tensor(out=shift[:, s, :], in0=moments[:, s, :, 0], scalar=-1.0,
                                               in1=rstd[:, s, :], op0=ALU.mult, op1=ALU.mult).then_inc(shift_done, 1)
                if again:
                    dve.wait_ge(stored[j % 4], (i + j // 4) * 16)
                for q in range(QUAD // 2):
                    sl = slice(q * P, (q + 1) * P)
                    ins = nc.vector.tensor_scalar(normed[:, j % 4, sl], res[:, s, sl], moments[:, s, q, 0:1],
                                                  rstd[:, s, q:q + 1], ALU.subtract, ALU.mult)
                ins.then_inc(norm_done, 1)

            def step(i, j, last=False, again=True):
                more = not beyond(j + 1, last)
                if more:
                    softplus(i, j + 1)
                if more:
                    residual(i, j + 1)
                normalise(i, j, again)

            dve.wait_ge(t["x_in"], 16 * nq)
            softplus(0, 0)
            residual(0, 0)
            for j in range(4):
                step(0, j, again=False)
            with dve.Fori(1, passes) as i:
                for j in range(4):
                    step(i, j)
            for j in range(rest):
                step(passes, j, last=True)


def schnet_block(nc, xT, x, dst_g, src_nat, src_col, dst_col, w_col, attrT, w_inT, b_in, w_fT, b_f, w_outT,
                 b_out, out):
    nodes = x.shape[0]
    groups = dst_g.shape[0]
    edges_pad = groups * GE
    nodes_pad = xT.shape[1]
    KA = QUAD * w_fT.shape[0] + 1
    assert nodes_pad >= nodes + P
    nq = -(-nodes // QE)
    tail = nodes - (nq - 1) * QE
    assert tail % QUAD == 0
    with ExitStack() as ctx:
        def sb(name, shape, dt=F32):
            return ctx.enter_context(nc.sbuf_tensor(f"{name}_sb", shape, dt))

        dram = dict(xT=xT, x=x, dst_g=dst_g, src_nat=src_nat, src_col=src_col, dst_col=dst_col,
                    w_col=w_col, attrT=attrT, w_inT=w_inT, b_in=b_in, w_fT=w_fT, b_f=b_f, w_outT=w_outT, b_out=b_out, out=out)
        first_cleared = ctx.enter_context(nc.semaphore("first_cleared_sem"))
        cleared = [ctx.enter_context(nc.semaphore(f"cleared{b}_sem")) for b in range(IN_FLIGHT)]
        x_in = ctx.enter_context(nc.semaphore("x_in_sem"))
        dram["h"] = nc.dram_tensor("h", (nodes_pad, P), F32, kind="Internal").ap()
        dram["rows"] = nc.dram_tensor("index_rows", (4, edges_pad), BF16, kind="Internal").ap()
        dram["bases"] = nc.dram_tensor("bases", (-(-groups // P) * P, 1), I32, kind="Internal").ap()
        dram["agg"] = [nc.dram_tensor(f"agg{r}", (nodes_pad, P), F32, kind="Internal").ap() for r in range(REPLICAS)]
        sbuf = dict(
            cols_all=sb("cols_all", [P, groups, COLS]),
            dst_all=sb("dst_all", [P, groups * GT], I32),
            attr=sb("attr", [KA, 2, GROUP * P]),
            ident=sb("ident", [P, P]),
            tri=sb("tri", [P, P]),
            w_f=sb("w_f", [KA, QE]),
            w_out=sb("w_out", [P, P]),
            b_out=sb("b_out", [1, P]),
            ones_row=sb("ones_row", [1, P]),
            zeros=sb("zeros", [P, nodes_pad // CHUNKS]),
            half=sb("half", [P, 1]),
            minus_half=sb("minus_half", [P, QUAD]),
            sel_src=sb("sel_src", [4, P], BF16),
            sel_dst=sb("sel_dst", [4, P], BF16),
            base_row=sb("base_row", [1, groups], I32),
            flag=sb("flag", [1, 1], I32),
        )
        t = dict(dram=dram, sbuf=sbuf, nodes=nodes, nodes_pad=nodes_pad, groups=groups, tiles=groups * GT,
                 first_cleared=first_cleared, cleared=cleared, nq=nq, tail=tail, x_in=x_in)
        prepare(nc, t)
        sbuf["x_all"] = sb("x_all", [P, nq, QE])
        edges(nc, t)
        finish(nc, t)


def layouts(x, src, dst, edge_attr_20, edge_weight, L0_gnn_W_in, L0_gnn_b_in, L0_gnn_W_f, L0_gnn_b_f, L0_gnn_W_out,
            L0_gnn_b_out):
    import numpy as np
    nodes, E = x.shape[0], src.shape[0]
    groups = -(-E // GE)
    pad = groups * GE - E
    nodes_pad = -(-(nodes + P) // (HS * QE)) * (HS * QE)
    src = np.pad(np.asarray(src), (0, pad), mode="edge")
    dst = np.pad(np.asarray(dst), (0, pad), mode="edge")
    w = np.pad(np.asarray(edge_weight), (0, pad))
    attr = np.pad(np.asarray(edge_attr_20), ((0, pad), (0, 0)))
    c = np.ascontiguousarray
    return {
        "xT": c(np.pad(np.asarray(x), ((0, nodes_pad - nodes), (0, 0))).T),
        "x": c(x),
        "dst_g": c(dst.reshape(groups, GE)),
        "src_nat": c(src.reshape(P, -1)),
        "src_col": c(src.reshape(-1, P).T),
        "dst_col": c(dst.reshape(-1, P).T),
        "w_col": c(w.reshape(-1, P).T),
        "attrT": c(attr.reshape(groups * GROUP, QUAD, P, -1).transpose(1, 3, 0, 2).reshape(-1, groups * GROUP * P)),
        "w_inT": c(np.asarray(L0_gnn_W_in).T),
        "b_in": c(np.tile(np.asarray(L0_gnn_b_in)[None, :], (P, 1))),
        "w_fT": c(np.asarray(L0_gnn_W_f).T),
        "b_f": c(np.asarray(L0_gnn_b_f)[None, :]),
        "w_outT": c(np.asarray(L0_gnn_W_out).T),
        "b_out": c(np.asarray(L0_gnn_b_out)[None, :]),
    }


def kernel(**inputs):
    import concourse.bacc as _bacc
    from concourse.bass_utils import run_bass_kernel_spmd as _run

    nc = _bacc.Bacc("TRN2", target_bir_lowering=False, num_devices=1)
    arrays = {f"in_{n}": a for n, a in layouts(**inputs).items()}
    args = [nc.dram_tensor(n, a.shape, mybir.dt.from_np(a.dtype), kind="ExternalInput").ap() for n, a in arrays.items()]
    out = nc.dram_tensor("out", inputs["x"].shape, F32, kind="ExternalOutput").ap()
    schnet_block(nc, *args, out)
    return _run(nc, [arrays], core_ids=[0]).results[0]["out"]
```
